# Optimizing a Trainium2 kernel written in Bass

```python
import numpy as np
import jax
import jax.numpy as jnp

def _softmax(x, axis=-1):
    return jax.nn.softmax(x, axis=axis)

def _gelu(x):
    return jax.nn.gelu(x, approximate=True)

def _silu(x):
    return jax.nn.silu(x)

def _sigmoid(x):
    return jax.nn.sigmoid(x)

def _layernorm(x, axis=-1, eps=1e-05):
    m = jnp.mean(x, axis=axis, keepdims=True)
    v = jnp.var(x, axis=axis, keepdims=True)
    return (x - m) / jnp.sqrt(v + eps)

def _scatter_add(tgt, idx, src, axis=0):
    return tgt.at[idx].add(src)

def _segment_sum(src, seg, n):
    return jax.ops.segment_sum(src, seg, n)
kernel_name = 'mk_vit_tower_cls_d1_tok_img1024_r4_49fee1'

def setup_inputs(seed: int=0):
    np.random.seed(seed)
    _w = jnp.asarray

    def _rec_inputs():
        import jax
        import jax.numpy as jnp
        _rk = jax.random.key(seed)
        x = -0.000348323 + 0.999952 * jax.random.normal(jax.random.fold_in(_rk, 1), (16, 3, 96, 96), jnp.float32)
        cls_tok = 0.02 * jax.random.normal(jax.random.fold_in(_rk, 5), (1, 1, 256), jnp.float32)
        return (x, cls_tok)
    x, cls_tok = _rec_inputs()

    def _L0_tok_setup():
        import jax, jax.numpy as jnp
        import numpy as np
        from jax import lax
        PATCH = 16
        key = jax.random.key(seed)
        k1, k2 = jax.random.split(key)
        B, C, IMG, HID = (32, 3, 96, 256)
        inputs = jax.random.normal(k1, (B, C, IMG, IMG), dtype=jnp.float32)
        flat = C * PATCH * PATCH
        W = jax.random.normal(k2, (flat, HID), dtype=jnp.float32) / np.sqrt(flat)
        return {'inputs': inputs, 'W': W}
    _L0_tok_all = _L0_tok_setup()
    _L0_tok_in = {k: v for k, v in _L0_tok_all.items() if k in ('W',)}
    del _L0_tok_all

    def _L0_attn_setup():
        import jax, jax.numpy as jnp
        import numpy as np
        import math
        N_HEAD = 16
        N_KV_HEAD = 4
        WINDOW = 128
        EPS = 1e-06

        def _rotate_half(t):
            t1, t2 = jnp.split(t, 2, axis=-1)
            return jnp.concatenate([-t2, t1], axis=-1)

        def _rope_tables(T, head_dim):
            theta = 1.0 / 10000.0 ** (jnp.arange(0, head_dim, 2, dtype=jnp.float32) / head_dim)
            pos = jnp.arange(T, dtype=jnp.float32)
            freqs = jnp.outer(pos, theta)
            cos = jnp.concatenate([jnp.cos(freqs), jnp.cos(freqs)], axis=-1)
            sin = jnp.concatenate([jnp.sin(freqs), jnp.sin(freqs)], axis=-1)
            return (cos, sin)
        key = jax.random.key(seed)
        k1, k2, k3, k4 = jax.random.split(key, 4)
        B, T, C = (1, 512, 256)
        kv_out = 2 * N_KV_HEAD * (C // N_HEAD)
        x = jax.random.normal(k1, (B, T, C), dtype=jnp.float32)
        Wq = jax.random.normal(k2, (C, C), dtype=jnp.float32) * 0.02
        Wkv = jax.random.normal(k3, (kv_out, C), dtype=jnp.float32) * 0.02
        Wproj = jax.random.normal(k4, (C, C), dtype=jnp.float32) * 0.02
        return {'x': x, 'Wq': Wq, 'Wkv': Wkv, 'Wproj': Wproj}
    _L0_attn_all = _L0_attn_setup()
    _L0_attn_in = {k: v for k, v in _L0_attn_all.items() if k in ('Wq', 'Wkv', 'Wproj')}
    del _L0_attn_all

    def _L0_ffn_setup():
        import jax, jax.numpy as jnp
        import numpy as np
        E = 8
        H = 256
        M = 512
        K = 2
        SE = 1
        BSZ, SEQ = (2, 256)
        W_SCALE = 0.02
        key = jax.random.key(seed)
        ks = jax.random.split(key, 9)
        return {'x': jax.random.normal(ks[0], (BSZ, SEQ, H), jnp.float32), 'gate_w': jax.random.normal(ks[1], (E, H), jnp.float32) * W_SCALE, 'beta': jnp.zeros((E,), jnp.float32), 'gate_proj_w': jax.random.normal(ks[2], (E, H, M), jnp.float32) * W_SCALE, 'up_proj_w': jax.random.normal(ks[3], (E, H, M), jnp.float32) * W_SCALE, 'down_proj_w': jax.random.normal(ks[4], (E, M, H), jnp.float32) * W_SCALE, 'shared_gate_w': jax.random.normal(ks[5], (SE, H, M), jnp.float32) * W_SCALE, 'shared_up_w': jax.random.normal(ks[6], (SE, H, M), jnp.float32) * W_SCALE, 'shared_down_w': jax.random.normal(ks[7], (SE, M, H), jnp.float32) * W_SCALE}
    _L0_ffn_all = _L0_ffn_setup()
    _L0_ffn_in = {k: v for k, v in _L0_ffn_all.items() if k in ('gate_w', 'beta', 'gate_proj_w', 'up_proj_w', 'down_proj_w', 'shared_gate_w', 'shared_up_w', 'shared_down_w')}
    del _L0_ffn_all
    return {'x': x, 'cls_tok': cls_tok, 'L0_tok_W': _L0_tok_in['W'], 'L0_attn_Wq': _L0_attn_in['Wq'], 'L0_attn_Wkv': _L0_attn_in['Wkv'], 'L0_attn_Wproj': _L0_attn_in['Wproj'], 'L0_ffn_gate_w': _L0_ffn_in['gate_w'], 'L0_ffn_beta': _L0_ffn_in['beta'], 'L0_ffn_gate_proj_w': _L0_ffn_in['gate_proj_w'], 'L0_ffn_up_proj_w': _L0_ffn_in['up_proj_w'], 'L0_ffn_down_proj_w': _L0_ffn_in['down_proj_w'], 'L0_ffn_shared_gate_w': _L0_ffn_in['shared_gate_w'], 'L0_ffn_shared_up_w': _L0_ffn_in['shared_up_w'], 'L0_ffn_shared_down_w': _L0_ffn_in['shared_down_w']}

def reference(x, cls_tok, L0_tok_W, L0_attn_Wq, L0_attn_Wkv, L0_attn_Wproj, L0_ffn_gate_w, L0_ffn_beta, L0_ffn_gate_proj_w, L0_ffn_up_proj_w, L0_ffn_down_proj_w, L0_ffn_shared_gate_w, L0_ffn_shared_up_w, L0_ffn_shared_down_w):
    import jax
    import jax.numpy as jnp

    def _L0_tok_ref(inputs, W):
        import jax, jax.numpy as jnp
        import numpy as np
        from jax import lax
        PATCH = 16
        B, C, H, Wimg = inputs.shape
        patches = lax.conv_general_dilated_patches(inputs, filter_shape=[PATCH, PATCH], window_strides=[PATCH, PATCH], padding='VALID', dimension_numbers=('NCHW', 'HWIO', 'NCHW'))
        patches = patches.reshape(B, -1, C * PATCH * PATCH)
        return jnp.einsum('bnf,fh->bnh', patches, W)

    def _L0_attn_ref(x, Wq, Wkv, Wproj):
        import jax, jax.numpy as jnp
        import numpy as np
        import math
        N_HEAD = 16
        N_KV_HEAD = 4
        WINDOW = 128
        EPS = 1e-06

        def _rotate_half(t):
            t1, t2 = jnp.split(t, 2, axis=-1)
            return jnp.concatenate([-t2, t1], axis=-1)

        def _rope_tables(T, head_dim):
            theta = 1.0 / 10000.0 ** (jnp.arange(0, head_dim, 2, dtype=jnp.float32) / head_dim)
            pos = jnp.arange(T, dtype=jnp.float32)
            freqs = jnp.outer(pos, theta)
            cos = jnp.concatenate([jnp.cos(freqs), jnp.cos(freqs)], axis=-1)
            sin = jnp.concatenate([jnp.sin(freqs), jnp.sin(freqs)], axis=-1)
            return (cos, sin)
        B, T, C = x.shape
        H, KV = (N_HEAD, N_KV_HEAD)
        d = C // H
        n_rep = H // KV
        q = (x @ Wq.T).reshape(B, T, H, d).transpose(0, 2, 1, 3)
        kv = x @ Wkv.T
        k, v = jnp.split(kv, 2, axis=2)
        k = k.reshape(B, T, KV, d).transpose(0, 2, 1, 3)
        v = v.reshape(B, T, KV, d).transpose(0, 2, 1, 3)
        q = q / (jnp.linalg.norm(q, axis=-1, keepdims=True) + EPS)
        k = k / (jnp.linalg.norm(k, axis=-1, keepdims=True) + EPS)
        cos, sin = _rope_tables(T, d)
        cos = cos[None, None]
        sin = sin[None, None]
        q = q * cos + _rotate_half(q) * sin
        k = k * cos + _rotate_half(k) * sin
        k = jnp.repeat(k, n_rep, axis=1)
        v = jnp.repeat(v, n_rep, axis=1)
        rows = jnp.arange(T)[:, None]
        cols = jnp.arange(T)[None, :]
        mask = (cols <= rows) & (cols > rows - WINDOW)
        scale = 1.0 / math.sqrt(d)
        scores = jnp.einsum('bhqd,bhkd->bhqk', q, k) * scale
        scores = jnp.where(mask[None, None], scores, -jnp.inf)
        attn = jax.nn.softmax(scores, axis=-1)
        y = jnp.einsum('bhqk,bhkd->bhqd', attn, v)
        y = y.transpose(0, 2, 1, 3).reshape(B, T, C)
        return y @ Wproj.T

    def _L0_ffn_ref(x, gate_w, beta, gate_proj_w, up_proj_w, down_proj_w, shared_gate_w, shared_up_w, shared_down_w):
        import jax, jax.numpy as jnp
        import numpy as np
        E = 8
        H = 256
        M = 512
        K = 2
        SE = 1
        BSZ, SEQ = (2, 256)
        W_SCALE = 0.02
        B0, S0, H0 = x.shape
        xt = x.reshape(-1, H0)
        B = xt.shape[0]
        logits = xt @ gate_w.T
        _, idx = jax.lax.top_k(logits + beta, K)
        probs = jax.nn.sigmoid(jnp.take_along_axis(logits, idx, axis=-1))
        c = jnp.zeros((B, E), xt.dtype).at[jnp.arange(B)[:, None], idx].add(probs)
        g = jnp.einsum('bh,ehm->bem', xt, gate_proj_w)
        u = jnp.einsum('bh,ehm->bem', xt, up_proj_w)
        h = jax.nn.silu(g) * u
        eo = jnp.einsum('bem,emh->beh', h, down_proj_w)
        combined = jnp.einsum('beh,be->bh', eo, c)
        sg = jnp.einsum('bh,ehm->bem', xt, shared_gate_w)
        su = jnp.einsum('bh,ehm->bem', xt, shared_up_w)
        sh = jax.nn.silu(sg) * su
        shared_out = jnp.einsum('bem,emh->beh', sh, shared_down_w).sum(axis=1)
        return (combined + shared_out).reshape(B0, S0, H0)
    h = _L0_tok_ref(x, L0_tok_W)
    h = jnp.concatenate([jnp.broadcast_to(cls_tok, (h.shape[0], 1, h.shape[2])), h], axis=1)
    h = h + _L0_attn_ref(_layernorm(h, axis=-1), L0_attn_Wq, L0_attn_Wkv, L0_attn_Wproj)
    h = h + _L0_ffn_ref(_layernorm(h, axis=-1), L0_ffn_gate_w, L0_ffn_beta, L0_ffn_gate_proj_w, L0_ffn_up_proj_w, L0_ffn_down_proj_w, L0_ffn_shared_gate_w, L0_ffn_shared_up_w, L0_ffn_shared_down_w)
    return h

_drawn_inputs = setup_inputs


def setup_inputs(seed=0):
    import zlib

    import numpy as np

    out = dict(_drawn_inputs(seed))
    spreads = {'L0_ffn_beta': (0.0, 0.634)}
    factors = {'cls_tok': 2.81,
     'L0_attn_Wq': 22.458,
     'L0_ffn_gate_w': 3.292,
     'L0_ffn_gate_proj_w': 2.745,
     'L0_ffn_up_proj_w': 2.722,
     'L0_ffn_down_proj_w': 2.72,
     'L0_ffn_shared_gate_w': 2.726,
     'L0_ffn_shared_up_w': 2.702,
     'L0_ffn_shared_down_w': 2.708}
    for name, (base, spread) in spreads.items():
        noise = np.random.default_rng([zlib.crc32(name.encode()), seed]).standard_normal(out[name].shape)
        drawn = base * np.exp(spread * noise) if base else spread * noise
        out[name] = jnp.asarray(drawn.astype(out[name].dtype))
    for name, factor in factors.items():
        out[name] = (out[name] * factor).astype(out[name].dtype)
    return out
```

```python
from contextlib import ExitStack

import concourse.bass as bass
import numpy as np
from concourse import mybir

F32 = mybir.dt.float32
F32R = mybir.dt.float32r
ALU = mybir.AluOpType
ACT = mybir.ActivationFunctionType
AX_X = mybir.AxisListType.X

P = 128
BATCH, CHANNELS, IMAGE, PATCH = 16, 3, 96, 16
HID = 256
PATCHES = (IMAGE // PATCH) ** 2
SEQ = PATCHES + 1
TOKENS = BATCH * SEQ
FLAT = CHANNELS * PATCH * PATCH
KF = FLAT // P
KH = HID // P
PER_GROUP = P // SEQ
T = PER_GROUP * SEQ
GROUPS = -(-BATCH // PER_GROUP)
PADDED = GROUPS * T
HEADS, KV, D = 16, 4, 16
REP = HEADS // KV
QKV = HID + 2 * KV * D
WIDE = 2 * D
EXPERTS, MID = 8, 512
TOP = 2
MT = MID // P
LN_EPS = 1e-5
QK_EPS = 1e-6
SCALE = 1.0 / D ** 0.5
HALF = TOKENS // 2
EXPERT_COLS = 3 * KH * MID
PIECES = 6
PIECE = EXPERT_COLS // PIECES
UNITS = 2 * MT
LAG = 2
HBUF = 4


def schedule():
    order = [("split_x", 0), ("embed", 0)]
    for i in range(GROUPS + 2):
        a, b, c = i, i - 1, i - 2
        steps = [("split_x", a + 1), ("norm_t", a), ("score0", b), ("attn_t", c), ("score1", b),
                 ("qkv", a), ("value0", b), ("project", c), ("score2", b), ("rope", a), ("value1", b),
                 ("score3", b), ("ffn_t", c), ("value2", b), ("embed", a + 1), ("stack", a),
                 ("value3", b), ("logits", c), ("heads_t", a), ("out_t", b)]
        order += [(s, g) for s, g in steps if 0 <= g < GROUPS]
    return order


def vit_block(nc, x, clsrows, w_tok, w_qkv, w_proj, w_gate, beta, w_exp, w_sh, cos, sin, mask, ident,
              before, c_dram, out):
    with ExitStack() as ctx:
        def sb(name, shape, dt=F32):
            return ctx.enter_context(nc.sbuf_tensor(name, shape, dt))

        def sem(name):
            return ctx.enter_context(nc.semaphore(name))

        banks = [ctx.enter_context(nc.psum_tensor(f"bank{i}", [P, 512], F32)) for i in range(8)]

        early_late = sb("early_late", [P, max(GROUPS * KF * T, EXPERTS * TOKENS)])
        xraw = early_late[:, 0:GROUPS * KF * T].rearrange("p (g k t) -> p g k t", g=GROUPS, k=KF)
        x_hi = [sb(f"x_hi{i}", [P, KF, T], F32R) for i in range(2)]
        x_lo = [sb(f"x_lo{i}", [P, KF, T], F32R) for i in range(2)]
        small_raw = sb("small_raw", [P, KF * HID + KH * (QKV + HID + EXPERTS)])
        small_hi = sb("small_hi", [P, KF * HID + KH * (QKV + HID + EXPERTS)], F32R)
        small_lo = sb("small_lo", [P, KF * HID + KH * (QKV + HID + EXPERTS)], F32R)
        cls_sb = sb("cls_sb", [T, HID])
        beta_sb = sb("beta_sb", [T, EXPERTS])
        cos_sb = sb("cos_sb", [T, D])
        sin_sb = sb("sin_sb", [T, D])
        mask_sb = sb("mask_sb", [T, T])
        id_sb = sb("id_sb", [P, P])
        before_sb = sb("before_sb", [T, EXPERTS, EXPERTS])

        def weights(t, at, k, n):
            return t[:, at:at + k * n].rearrange("p (k n) -> p k n", k=k)

        at_qkv = KF * HID
        at_proj = at_qkv + KH * QKV
        at_gate = at_proj + KH * HID
        tok_w = [weights(t, 0, KF, HID) for t in (small_hi, small_lo)]
        qkv_w = [weights(t, at_qkv, KH, QKV) for t in (small_hi, small_lo)]
        proj_w = [weights(t, at_proj, KH, HID) for t in (small_hi, small_lo)]
        gate_w = [weights(t, at_gate, KH, EXPERTS) for t in (small_hi, small_lo)]

        h_all = sb("h_all", [T, GROUPS, HID])
        stats = sb("stats", [T, 2, 6])
        moments = sb("moments", [T, 2, 2])
        rstd = sb("rstd", [T, 2])
        xn = sb("xn", [T, HID])
        xnT_hi = sb("xnT_hi", [P, KH, T], F32R)
        xnT_lo = sb("xnT_lo", [P, KH, T], F32R)
        squares = sb("squares", [T, HEADS + KV, D])
        norm2 = sb("norm2", [T, HEADS + KV])
        root = sb("root", [T, HEADS + KV])
        norm = sb("norm", [T, HEADS + KV])
        powers = sb("powers", [T, 2, HEADS + KV])
        variance = sb("variance", [T, 2])
        inv_norm = sb("inv_norm", [T, HEADS + KV])
        qkn = sb("qkn", [T, HEADS + KV, D])
        turned = sb("turned", [T, HEADS + KV, D])
        rot = sb("rot", [T, HEADS + KV, D])
        heads = sb("heads", [T, HEADS + 2 * KV, WIDE])
        v_one = [sb(f"v_one{i}", [T, KV, WIDE]) for i in range(2)]
        qT = sb("qT", [P, REP * T], F32R)
        kT = sb("kT", [P, 2, T], F32R)
        exps = [sb(f"exps{i}", [T, REP, T]) for i in range(2)]
        probs = [sb(f"probs{i}", [T, REP, T]) for i in range(2)]
        oT = sb("oT", [P, REP * T])
        inv_den = sb("inv_den", [T, HEADS])
        attn = sb("attn", [T, HEADS, D])
        attnT_hi = sb("attnT_hi", [P, KH, T], F32R)
        attnT_lo = sb("attnT_lo", [P, KH, T], F32R)
        xn2 = sb("xn2", [T, HID])
        x2_hi = sb("x2_hi", [P, KH, PADDED], F32R)
        x2_lo = sb("x2_lo", [P, KH, PADDED], F32R)
        logits = sb("logits", [T, GROUPS, EXPERTS])
        biased = sb("biased", [T, GROUPS, EXPERTS])

        greater = sb("greater", [T, GROUPS, EXPERTS * EXPERTS])
        equal = sb("equal", [T, GROUPS, EXPERTS * EXPERTS])
        rank = sb("rank", [T, GROUPS, EXPERTS])
        expneg = sb("expneg", [T, GROUPS, EXPERTS])
        sigm = sb("sigm", [T, GROUPS, EXPERTS])
        coef = sb("coef", [T, GROUPS, EXPERTS])
        coefT = sb("coefT", [EXPERTS, PADDED])
        cbc = early_late[:, 0:EXPERTS * TOKENS].rearrange("p (e t) -> p e t", e=EXPERTS)

        wraw = [sb(f"wraw{i}", [P, EXPERT_COLS]) for i in range(2)]
        w_hi = [sb(f"w_hi{i}", [P, EXPERT_COLS], F32R) for i in range(2)]
        w_lo = [sb(f"w_lo{i}", [P, EXPERT_COLS], F32R) for i in range(2)]
        silu = [sb(f"silu{i}", [P, HALF]) for i in range(2)]
        upc = [sb(f"upc{i}", [P, HALF]) for i in range(2)]
        mid = [sb(f"mid{i}", [P, HALF]) for i in range(2)]
        mid_hi = sb("mid_hi", [P, HBUF, HALF], F32R)
        mid_lo = sb("mid_lo", [P, HBUF, HALF], F32R)
        result = small_raw[:, 0:KH * TOKENS].rearrange("p (k t) -> p k t", k=KH)

        def gate_up(t, matrix, k, m):
            at = (matrix * KH + k) * MID + m * P
            return t[:, at:at + P]

        def down(t, m, hid):
            at = 2 * KH * MID + m * HID + hid * P
            return t[:, at:at + P]

        ps_embed = banks[0][0:T, 0:HID]
        ps_proj = banks[0][0:T, HID:2 * HID]
        ps_xnT = banks[1][:, 0:KH * T]
        ps_attnT = banks[1][:, 256:256 + KH * T]
        ps_qkv = banks[2][0:T, 0:QKV]
        ps_logit = banks[2][0:T, QKV:QKV + EXPERTS]
        ps_qT = banks[3][:, 0:REP * T]
        ps_out = banks[3][0:T, :]
        ps_kT = banks[4][:, 0:2 * T]
        ps_x2T = banks[4][:, 256:256 + KH * T]
        ps_score = [banks[5][0:T, 0:REP * T], banks[6][0:T, 0:REP * T]]
        ps_value = banks[7][:, 0:REP * T]
        ps_gate = [banks[0][:, 0:HALF], banks[1][:, 0:HALF]]
        ps_up = [banks[2][:, 0:HALF], banks[3][:, 0:HALF]]
        ps_y = [[banks[4 + 2 * c + hid][:, 0:HALF] for hid in range(KH)] for c in range(2)]

        d_x = [sem(f"d_x{g}") for g in range(GROUPS)]
        d_tok = sem("d_tok")
        d_small = sem("d_small")
        d_const = sem("d_const")
        d_shared = sem("d_shared")
        d_expert = [sem("d_expert0"), sem("d_expert1")]
        d_coef = sem("d_coef")
        d_cbc = sem("d_cbc")
        d_out = sem("d_out")

        ws_hi = sem("ws_hi")
        ws_lo = sem("ws_lo")
        fill = sem("fill")
        xs_hi = sem("xs_hi")
        xs_lo = sem("xs_lo")
        embedded = sem("embedded")
        h_ready = sem("h_ready")
        xn_ready = sem("xn_ready")
        var_ready = [sem("var_ready0"), sem("var_ready1")]
        rstd_ready = [sem("rstd_ready0"), sem("rstd_ready1")]
        norm2_ready = sem("norm2_ready")
        root_ready = sem("root_ready")
        powers_set = sem("powers_set")
        xnT_ps = sem("xnT_ps")
        xnT_h = sem("xnT_h")
        xnT_l = sem("xnT_l")
        qkv_ps = sem("qkv_ps")
        sq_ready = sem("sq_ready")
        v_ready = sem("v_ready")
        qkn_ready = sem("qkn_ready")
        turned_ready = sem("turned_ready")
        rot_ready = sem("rot_ready")
        heads_h = sem("heads_h")
        heads_l = sem("heads_l")
        heads_ps = sem("heads_ps")
        qT_ready = sem("qT_ready")
        kT_ready = sem("kT_ready")
        score_ps = sem("score_ps")
        exp_ready = sem("exp_ready")
        prob_ready = sem("prob_ready")
        value_ps = sem("value_ps")
        oT_ready = sem("oT_ready")
        out_ps = sem("out_ps")
        attn_ready = sem("attn_ready")
        attnT_ps = sem("attnT_ps")
        attnT_h = sem("attnT_h")
        attnT_l = sem("attnT_l")
        proj_ps = sem("proj_ps")
        h2_ready = sem("h2_ready")
        xn2_ready = sem("xn2_ready")
        x2T_ps = sem("x2T_ps")
        x2_h = sem("x2_h")
        x2_l = sem("x2_l")
        logit_ps = sem("logit_ps")
        logit_ready = sem("logit_ready")
        expneg_ready = sem("expneg_ready")
        coef_ready = sem("coef_ready")
        coefT_ps = sem("coefT_ps")
        coefT_ready = sem("coefT_ready")
        dve_step = sem("dve_step")
        we_hi = sem("we_hi")
        we_lo = sem("we_lo")
        gu_ps = sem("gu_ps")
        silu_ready = sem("silu_ready")
        up_read = sem("up_read")
        mid_ready = sem("mid_ready")
        mid_h = sem("mid_h")
        mid_l = sem("mid_l")
        downed = sem("downed")
        y_ready = sem("y_ready")

        block = ctx.enter_context(nc.Block())
        ORDER = schedule()
        CONSTS = 7

        @block.sync
        def _(sp):
            n_tok = KF * HID
            sp.dma_start(xraw[:, 0], x[:, 0]).then_inc(d_x[0], 16)
            sp.dma_start(small_raw[:, 0:n_tok], w_tok).then_inc(d_tok, 16)
            sp.dma_start(small_raw[:, at_qkv:at_proj], w_qkv).then_inc(d_small, 16)
            for g in range(1, GROUPS):
                sp.dma_start(xraw[:, g], x[:, g]).then_inc(d_x[g], 16)
                if g == 1:
                    sp.dma_start(small_raw[:, at_proj:at_gate], w_proj).then_inc(d_small, 16)
                    sp.dma_start(small_raw[:, at_gate:], w_gate).then_inc(d_small, 16)
            sp.dma_start(wraw[0][:], w_sh).then_inc(d_shared, 16)
            sp.dma_start(wraw[1][:], w_exp[0]).then_inc(d_expert[0], 16)
            sp.wait_ge(coefT_ready, GROUPS)
            sp.dma_start(c_dram, coefT[:, 0:TOKENS]).then_inc(d_coef, 16)
            sp.wait_ge(d_coef, 16)
            sp.dma_start(cbc, c_dram.partition_broadcast(P)).then_inc(d_cbc, 16)
            for e in range(1, EXPERTS):
                sp.wait_ge(we_lo, PIECES * e)
                sp.dma_start(wraw[(e + 1) % 2][:], w_exp[e]).then_inc(d_expert[e % 2], 16)
            for hid in range(KH):
                sp.wait_ge(y_ready, 2 * hid + 2)
                sp.dma_start(out[hid * P:(hid + 1) * P, :], result[:, hid]).then_inc(d_out, 16)
            sp.wait_ge(d_out, 16 * KH)

        @block.gpsimd
        def _(pool):
            pool.dma_start(cls_sb[:], clsrows).then_inc(d_const, 16)
            pool.dma_start(id_sb[:], ident).then_inc(d_const, 16)
            pool.dma_start(cos_sb[:], cos).then_inc(d_const, 16)
            pool.dma_start(sin_sb[:], sin).then_inc(d_const, 16)
            pool.dma_start(mask_sb[:], mask).then_inc(d_const, 16)
            pool.dma_start(before_sb[:], before).then_inc(d_const, 16)
            pool.dma_start(beta_sb[:], beta.partition_broadcast(T)).then_inc(d_const, 16)
            pool.wait_ge(d_const, 16 * CONSTS)
            pool.wait_ge(powers_set, 2)

            def inverse_root(g, which):
                pool.wait_ge(var_ready[which], g + 1)
                nc.gpsimd.tensor_tensor(rstd[:, which:which + 1], variance[:, which:which + 1],
                                        powers[:, 1, 0:1], ALU.pow).then_inc(rstd_ready[which], 1)

            for step, g in ORDER:
                if step == "embed":
                    inverse_root(g, 0)
                elif step == "project":
                    inverse_root(g, 1)
                elif step == "qkv":
                    pool.wait_ge(norm2_ready, g + 1)
                    nc.gpsimd.tensor_tensor(root[:], norm2[:], powers[:, 0], ALU.pow).then_inc(root_ready, 1)
                elif step == "split_x":
                    pool.wait_ge(xs_hi, g + 1)
                    if g >= 2:
                        pool.wait_ge(embedded, g - 1)
                    nc.gpsimd.tensor_tensor(x_lo[g % 2][:], xraw[:, g], x_hi[g % 2][:].bitcast(F32),
                                            ALU.subtract).then_inc(xs_lo, 1)
                elif step == "rope":
                    pool.wait_ge(qkn_ready, g + 1)
                    if g >= 1:
                        pool.wait_ge(rot_ready, g)
                    nc.gpsimd.tensor_tensor(
                        turned[:, :, 0:D // 2], qkn[:, :, D // 2:D],
                        sin_sb[:, None, 0:D // 2].broadcast_to([T, HEADS + KV, D // 2]), ALU.mult)
                    nc.gpsimd.tensor_tensor(
                        turned[:, :, D // 2:D], qkn[:, :, 0:D // 2],
                        sin_sb[:, None, D // 2:D].broadcast_to([T, HEADS + KV, D // 2]),
                        ALU.mult).then_inc(turned_ready, 1)
                elif step.startswith("score"):
                    n = g * KV + int(step[-1])
                    pool.wait_ge(exp_ready, n + 1)
                    if n >= 2:
                        pool.wait_ge(value_ps, n - 1)
                    nc.gpsimd.tensor_tensor(probs[n % 2][:], exps[n % 2][:],
                                            mask_sb[:, None, :].broadcast_to([T, REP, T]),
                                            ALU.mult).then_inc(prob_ready, 1)

        @block.scalar
        def _(act):
            def copy(dst, src):
                return nc.scalar.activation(dst, src, ACT.Copy)

            act.wait_ge(d_tok, 16)
            copy(small_hi[:, 0:at_qkv], small_raw[:, 0:at_qkv]).then_inc(ws_hi, 1)

            for step, g in ORDER:
                if step == "split_x":
                    act.wait_ge(d_x[g], 16)
                    if g >= 2:
                        act.wait_ge(embedded, g - 1)
                    copy(x_hi[g % 2][:], xraw[:, g]).then_inc(xs_hi, 1)
                    if g == 0:
                        act.wait_ge(d_small, 48)
                        copy(small_hi[:, at_qkv:], small_raw[:, at_qkv:]).then_inc(ws_hi, 1)
                elif step == "norm_t":
                    act.wait_ge(xnT_ps, g + 1)
                    if g >= 1:
                        act.wait_ge(qkv_ps, g)
                    copy(xnT_hi[:].rearrange("p k t -> p (k t)"), ps_xnT).then_inc(xnT_h, 1)
                elif step == "qkv":
                    act.wait_ge(qkv_ps, g + 1)
                    if g >= 1:
                        act.wait_ge(qkn_ready, g)
                    nc.scalar.activation(squares[:].rearrange("p h d -> p (h d)"),
                                         ps_qkv[:, 0:HID + KV * D], ACT.Square).then_inc(sq_ready, 1)
                    if g == 0:
                        act.wait_ge(fill, 2)
                    if g >= 2:
                        act.wait_ge(value_ps, KV * (g - 1))
                    copy(v_one[g % 2][:, :, 0:D],
                         ps_qkv[:, HID + KV * D:QKV].rearrange("p (j d) -> p j d", j=KV)).then_inc(v_ready, 1)
                elif step == "stack":
                    act.wait_ge(rot_ready, g + 1)
                    if g >= 1:
                        act.wait_ge(heads_ps, g)
                    hr = heads[:].bitcast(F32R)
                    copy(hr[:, 0:HEADS, 0:D], rot[:, 0:HEADS])
                    k4 = hr[:, HEADS:HEADS + KV].rearrange("p j (two d) -> p j two d", two=2)
                    copy(k4, rot[:, HEADS:HEADS + KV, None, :].broadcast_to([T, KV, 2, D])).then_inc(heads_h, 1)
                elif step == "heads_t":
                    act.wait_ge(heads_ps, g + 1)
                    if g >= 1:
                        act.wait_ge(score_ps, KV * g)
                    copy(qT[:], ps_qT).then_inc(qT_ready, 1)
                elif step.startswith("score"):
                    n = g * KV + int(step[-1])
                    act.wait_ge(score_ps, n + 1)
                    if n >= 2:
                        act.wait_ge(prob_ready, n - 1)
                    nc.scalar.activation(exps[n % 2][:].rearrange("p r t -> p (r t)"), ps_score[n % 2],
                                         ACT.Exp, scale=SCALE).then_inc(exp_ready, 1)
                elif step == "out_t":
                    act.wait_ge(value_ps, KV * (g + 1))
                    if g >= 1:
                        act.wait_ge(out_ps, g)
                    copy(oT[:], ps_value).then_inc(oT_ready, 1)
                elif step == "attn_t":
                    act.wait_ge(attnT_ps, g + 1)
                    if g >= 1:
                        act.wait_ge(proj_ps, g)
                    copy(attnT_hi[:].rearrange("p k t -> p (k t)"), ps_attnT).then_inc(attnT_h, 1)
                elif step == "ffn_t":
                    act.wait_ge(x2T_ps, g + 1)
                    copy(x2_hi[:, :, g * T:(g + 1) * T],
                         ps_x2T.rearrange("p (k t) -> p k t", k=KH)).then_inc(x2_h, 1)
            act.wait_ge(logit_ready, GROUPS)
            nc.scalar.activation(expneg[:], logits[:], ACT.Exp, scale=-1.0).then_inc(expneg_ready, 1)

            def weights_hi(e, piece):
                at = slice(piece * PIECE, (piece + 1) * PIECE)
                b = e % 2
                copy(w_hi[b][:, at], wraw[b][:, at]).then_inc(we_hi, 1)

            act.wait_ge(d_shared, 16)
            for piece in range(PIECES):
                weights_hi(0, piece)

            for e in range(EXPERTS + 1):
                for unit in range(UNITS):
                    u = e * UNITS + unit
                    act.wait_ge(gu_ps, u + 1)
                    if u >= 2:
                        act.wait_ge(mid_ready, u - 1)
                    nc.scalar.activation(silu[u % 2][:], ps_gate[u % 2], ACT.Silu).then_inc(silu_ready, 1)
                    if e < EXPERTS and unit >= LAG:
                        piece = unit - LAG
                        if piece == 0:
                            act.wait_ge(d_expert[e % 2], 16 * (e // 2 + 1))
                            act.wait_ge(downed, u - LAG)
                        weights_hi(e + 1, piece)
                    act.wait_ge(mid_ready, u + 1)
                    if u >= HBUF:
                        act.wait_ge(downed, u - HBUF + 1)
                    copy(mid_hi[:, u % HBUF], mid[u % 2][:]).then_inc(mid_h, 1)

        @block.vector
        def _(dve):
            steps = [0]

            def settle(ins):
                steps[0] += 1
                ins.then_inc(dve_step, 1)
                dve.wait_ge(dve_step, steps[0])

            def layernorm(g, src, which, dst, ready):
                settle(nc.vector.bn_stats(stats[:, which], src))
                settle(nc.vector.bn_aggr(moments[:, which], stats[:, which]))
                nc.vector.tensor_scalar(variance[:, which:which + 1], moments[:, which, 1:2], LN_EPS, None,
                                        ALU.add).then_inc(var_ready[which], 1)
                dve.wait_ge(rstd_ready[which], g + 1)
                nc.vector.tensor_scalar(dst, src, moments[:, which, 0:1], rstd[:, which:which + 1],
                                        ALU.subtract, ALU.mult).then_inc(ready, 1)

            for i in range(2):
                settle(nc.vector.memset(v_one[i][:, :, D:WIDE], 0.0))
            nc.vector.memset(powers[:, 0], 0.5).then_inc(powers_set, 1)
            nc.vector.memset(powers[:, 1], -0.5).then_inc(powers_set, 1)
            for i in range(2):
                nc.vector.memset(v_one[i][:, :, D:D + 1], 1.0).then_inc(fill, 1)
            dve.wait_ge(ws_hi, 1)
            nc.vector.tensor_tensor(small_lo[:, 0:at_qkv], small_raw[:, 0:at_qkv],
                                    small_hi[:, 0:at_qkv].bitcast(F32), ALU.subtract).then_inc(ws_lo, 1)
            for step, g in ORDER:
                if step == "split_x" and g == 1:
                    dve.wait_ge(ws_hi, 2)
                    nc.vector.tensor_tensor(small_lo[:, at_qkv:], small_raw[:, at_qkv:],
                                            small_hi[:, at_qkv:].bitcast(F32), ALU.subtract).then_inc(ws_lo, 1)
                elif step == "embed":
                    if g == 0:
                        dve.wait_ge(d_const, 16 * CONSTS)
                    dve.wait_ge(embedded, g + 1)
                    settle(nc.vector.tensor_tensor(h_all[:, g], ps_embed, cls_sb[:], ALU.add))
                    if g >= 1:
                        dve.wait_ge(xnT_ps, g)
                    layernorm(g, h_all[:, g], 0, xn[:], xn_ready)
                elif step == "norm_t":
                    dve.wait_ge(xnT_h, g + 1)
                    nc.vector.tensor_tensor(xnT_lo[:].rearrange("p k t -> p (k t)"), ps_xnT,
                                            xnT_hi[:].rearrange("p k t -> p (k t)").bitcast(F32),
                                            ALU.subtract).then_inc(xnT_l, 1)
                elif step == "qkv":
                    dve.wait_ge(sq_ready, g + 1)
                    nc.vector.reduce_sum(norm2[:], squares[:], AX_X).then_inc(norm2_ready, 1)
                    dve.wait_ge(root_ready, g + 1)
                    settle(nc.vector.tensor_scalar(norm[:], root[:], QK_EPS, None, ALU.add))
                    settle(nc.vector.reciprocal(inv_norm[:], norm[:]))
                    if g >= 1:
                        dve.wait_ge(turned_ready, g)
                    dve.wait_ge(v_ready, g + 1)
                    nc.vector.tensor_tensor(
                        qkn[:], ps_qkv[:, 0:HID + KV * D].rearrange("p (h d) -> p h d", d=D),
                        inv_norm[:, :, None].broadcast_to([T, HEADS + KV, D]), ALU.mult).then_inc(qkn_ready, 1)
                elif step == "rope":
                    if g >= 1:
                        dve.wait_ge(heads_l, g)
                    dve.wait_ge(qkn_ready, g + 1)
                    settle(nc.vector.tensor_tensor(rot[:], qkn[:],
                                                   cos_sb[:, None, :].broadcast_to([T, HEADS + KV, D]), ALU.mult))
                    dve.wait_ge(turned_ready, g + 1)
                    nc.vector.tensor_tensor(rot[:], rot[:], turned[:], ALU.add).then_inc(rot_ready, 1)
                elif step == "stack":
                    dve.wait_ge(heads_h, g + 1)
                    nc.vector.tensor_tensor(heads[:, 0:HEADS, D:WIDE], rot[:, 0:HEADS], heads[:, 0:HEADS, 0:D],
                                            ALU.subtract)
                    k4 = heads[:, HEADS + KV:].rearrange("p j (two d) -> p j two d", two=2)
                    h4 = heads[:, HEADS:HEADS + KV].rearrange("p j (two d) -> p j two d", two=2)
                    nc.vector.tensor_tensor(k4, rot[:, HEADS:HEADS + KV, None, :].broadcast_to([T, KV, 2, D]),
                                            h4, ALU.subtract).then_inc(heads_l, 1)
                elif step == "heads_t":
                    dve.wait_ge(heads_ps, g + 1)
                    if g >= 1:
                        dve.wait_ge(score_ps, KV * g)
                    nc.vector.tensor_copy(kT[:].rearrange("p k t -> p (k t)"), ps_kT).then_inc(kT_ready, 1)
                elif step == "out_t":
                    dve.wait_ge(out_ps, g + 1)
                    o4 = ps_out.rearrange("p (h w) -> p h w", w=WIDE)
                    settle(nc.vector.reciprocal(inv_den[:, :, None], o4[:, :, D:D + 1]))
                    if g >= 1:
                        dve.wait_ge(attnT_ps, g)
                    nc.vector.tensor_tensor(attn[:], o4[:, :, 0:D],
                                            inv_den[:, :, None].broadcast_to([T, HEADS, D]),
                                            ALU.mult).then_inc(attn_ready, 1)
                elif step == "attn_t":
                    dve.wait_ge(attnT_h, g + 1)
                    nc.vector.tensor_tensor(attnT_lo[:].rearrange("p k t -> p (k t)"), ps_attnT,
                                            attnT_hi[:].rearrange("p k t -> p (k t)").bitcast(F32),
                                            ALU.subtract).then_inc(attnT_l, 1)
                elif step == "project":
                    dve.wait_ge(proj_ps, g + 1)
                    settle(nc.vector.tensor_tensor(h_all[:, g], h_all[:, g], ps_proj, ALU.add))
                    if g >= 1:
                        dve.wait_ge(x2T_ps, g)
                    layernorm(g, h_all[:, g], 1, xn2[:], xn2_ready)
                elif step == "ffn_t":
                    dve.wait_ge(x2_h, g + 1)
                    at = slice(g * T, (g + 1) * T)
                    nc.vector.tensor_tensor(x2_lo[:, :, at], ps_x2T.rearrange("p (k t) -> p k t", k=KH),
                                            x2_hi[:, :, at].bitcast(F32), ALU.subtract).then_inc(x2_l, 1)
                elif step == "logits":
                    dve.wait_ge(logit_ps, g + 1)
                    nc.vector.tensor_copy(logits[:, g], ps_logit)
                    nc.vector.tensor_tensor(biased[:, g], ps_logit, beta_sb[:], ALU.add).then_inc(logit_ready, 1)

            dve.wait_ge(logit_ready, GROUPS)
            for g in range(GROUPS):
                shape = [T, EXPERTS, EXPERTS]
                mine = biased[:, g, :, None].broadcast_to(shape)
                other = biased[:, g, None, :].broadcast_to(shape)
                gr = greater[:, g].rearrange("p (e f) -> p e f", f=EXPERTS)
                eq = equal[:, g].rearrange("p (e f) -> p e f", f=EXPERTS)
                nc.vector.tensor_tensor(gr, other, mine, ALU.is_gt)
                nc.vector.tensor_tensor(eq, other, mine, ALU.is_equal).then_inc(dve_step, 1)
                steps[0] += 1
            dve.wait_ge(dve_step, steps[0])
            settle(nc.vector.tensor_tensor(
                equal[:], equal[:], before_sb[:].rearrange("p e f -> p (e f)")[:, None, :].broadcast_to(
                    [T, GROUPS, EXPERTS * EXPERTS]), ALU.mult))
            settle(nc.vector.tensor_tensor(greater[:], greater[:], equal[:], ALU.add))
            settle(nc.vector.reduce_sum(rank[:], greater[:].rearrange("p g (e f) -> p g e f", f=EXPERTS), AX_X))
            dve.wait_ge(expneg_ready, 1)
            settle(nc.vector.tensor_scalar(expneg[:], expneg[:], 1.0, None, ALU.add))
            settle(nc.vector.reciprocal(sigm[:], expneg[:]))
            nc.vector.scalar_tensor_tensor(coef[:], rank[:], TOP - 0.5, sigm[:], ALU.is_lt,
                                           ALU.mult).then_inc(coef_ready, 1)
            for g in range(GROUPS):
                dve.wait_ge(coefT_ps, g + 1)
                nc.vector.tensor_copy(coefT[:, g * T:(g + 1) * T],
                                      banks[g % 2][0:EXPERTS, 0:T]).then_inc(coefT_ready, 1)

            def weights_lo(e, piece):
                at = slice(piece * PIECE, (piece + 1) * PIECE)
                b = e % 2
                dve.wait_ge(we_hi, e * PIECES + piece + 1)
                nc.vector.tensor_tensor(w_lo[b][:, at], wraw[b][:, at], w_hi[b][:, at].bitcast(F32),
                                        ALU.subtract).then_inc(we_lo, 1)

            for piece in range(PIECES):
                weights_lo(0, piece)

            for e in range(EXPERTS + 1):
                for unit in range(UNITS):
                    u = e * UNITS + unit
                    chunk = slice((unit // MT) * HALF, (unit // MT + 1) * HALF)
                    dve.wait_ge(gu_ps, u + 1)
                    if e == 0:
                        dve.wait_ge(silu_ready, u + 1)
                        if u >= 2:
                            dve.wait_ge(mid_h, u - 1)
                        nc.vector.tensor_tensor(mid[u % 2][:], ps_up[u % 2], silu[u % 2][:],
                                                ALU.mult).then_inc(mid_ready, 1)
                    else:
                        if u == UNITS:
                            dve.wait_ge(d_cbc, 16)
                        nc.vector.tensor_tensor(upc[u % 2][:], ps_up[u % 2], cbc[:, e - 1, chunk],
                                                ALU.mult).then_inc(up_read, 1)
                        dve.wait_ge(silu_ready, u + 1)
                        dve.wait_ge(up_read, u - UNITS + 1)
                        dve.wait_ge(mid_h, u - 1)
                        nc.vector.tensor_tensor(mid[u % 2][:], upc[u % 2][:], silu[u % 2][:],
                                                ALU.mult).then_inc(mid_ready, 1)
                    if e < EXPERTS and unit >= LAG:
                        weights_lo(e + 1, unit - LAG)
                    dve.wait_ge(mid_h, u + 1)
                    nc.vector.tensor_tensor(mid_lo[:, u % HBUF], mid[u % 2][:], mid_hi[:, u % HBUF].bitcast(F32),
                                            ALU.subtract).then_inc(mid_l, 1)
            dve.wait_ge(downed, (EXPERTS + 1) * UNITS)
            for hid in range(KH):
                for c in range(2):
                    nc.vector.tensor_copy(result[:, hid, c * HALF:(c + 1) * HALF], ps_y[c][hid]).then_inc(y_ready, 1)

        @block.tensor
        def _(pe):
            def product(dst, pairs):
                for i, (left, right) in enumerate(pairs):
                    last = nc.tensor.matmul(dst, left, right, start=(i == 0), stop=(i == len(pairs) - 1))
                return last

            def split(chunks, left, right):
                return [(left[a](k), right[b](k)) for k in range(chunks) for a, b in ((0, 0), (0, 1), (1, 0))]

            pe.wait_ge(d_const, 16 * CONSTS)
            for step, g in ORDER:
                if step == "embed":
                    if g == 0:
                        pe.wait_ge(ws_lo, 1)
                    else:
                        pe.wait_ge(xn_ready, g)
                    if g >= 3:
                        pe.wait_ge(xn2_ready, g - 2)
                    pe.wait_ge(xs_lo, g + 1)
                    xh, xl = x_hi[g % 2], x_lo[g % 2]
                    product(ps_embed, split(KF, (lambda k: xh[:, k], lambda k: xl[:, k]),
                                            (lambda k: tok_w[0][:, k], lambda k: tok_w[1][:, k]))
                            ).then_inc(embedded, 1)
                elif step == "norm_t":
                    pe.wait_ge(xn_ready, g + 1)
                    if g >= 1:
                        pe.wait_ge(xnT_l, g)
                    if g >= 3:
                        pe.wait_ge(attnT_l, g - 2)
                    for k in range(KH):
                        last = nc.tensor.transpose(ps_xnT[:, k * T:(k + 1) * T], xn[:, k * P:(k + 1) * P],
                                                   id_sb[0:T, 0:T])
                    last.then_inc(xnT_ps, 1)
                elif step == "qkv":
                    if g == 0:
                        pe.wait_ge(ws_lo, 2)
                    else:
                        pe.wait_ge(qkn_ready, g)
                        pe.wait_ge(v_ready, g)
                    if g >= 3:
                        pe.wait_ge(logit_ready, g - 2)
                    pe.wait_ge(xnT_l, g + 1)
                    product(ps_qkv, split(KH, (lambda k: xnT_hi[:, k], lambda k: xnT_lo[:, k]),
                                          (lambda k: qkv_w[0][:, k], lambda k: qkv_w[1][:, k]))
                            ).then_inc(qkv_ps, 1)
                elif step == "heads_t":
                    pe.wait_ge(heads_l, g + 1)
                    if g >= 1:
                        pe.wait_ge(kT_ready, g)
                    if g >= 2:
                        pe.wait_ge(attn_ready, g - 1)
                        pe.wait_ge(x2_l, g - 1)
                    blocks = heads[:].rearrange("p (b j) w -> p b (j w)", j=KV)
                    for b in range(REP + 2):
                        dst = ps_qT if b < REP else ps_kT
                        at = (b % REP) * T
                        last = nc.tensor.transpose(dst[:, at:at + T], blocks[:, b], id_sb[0:T, 0:T])
                    last.then_inc(heads_ps, 1)
                elif step.startswith("score"):
                    j = int(step[-1])
                    n = g * KV + j
                    if j == 0:
                        pe.wait_ge(qT_ready, g + 1)
                        pe.wait_ge(kT_ready, g + 1)
                    if n >= 2:
                        pe.wait_ge(exp_ready, n - 1)
                    rows = slice(WIDE * j, WIDE * (j + 1))
                    product(ps_score[n % 2], [(kT[rows, half], qT[rows, :]) for half in range(2)]
                            ).then_inc(score_ps, 1)
                elif step.startswith("value"):
                    j = int(step[-1])
                    n = g * KV + j
                    if j == 0:
                        pe.wait_ge(v_ready, g + 1)
                        if g >= 1:
                            pe.wait_ge(oT_ready, g)
                    pe.wait_ge(prob_ready, n + 1)
                    nc.tensor.matmul(ps_value[WIDE * j:WIDE * (j + 1), :], v_one[g % 2][:, j],
                                     probs[n % 2][:].rearrange("p r t -> p (r t)"), start=True,
                                     stop=True).then_inc(value_ps, 1)
                elif step == "out_t":
                    pe.wait_ge(oT_ready, g + 1)
                    if g + 1 < GROUPS:
                        pe.wait_ge(qT_ready, g + 2)
                    for r in range(REP):
                        last = nc.tensor.transpose(ps_out[:, r * P:(r + 1) * P], oT[:, r * T:(r + 1) * T], id_sb[:])
                    last.then_inc(out_ps, 1)
                elif step == "attn_t":
                    pe.wait_ge(attn_ready, g + 1)
                    if g >= 1:
                        pe.wait_ge(attnT_l, g)
                    pe.wait_ge(xnT_l, min(g + 3, GROUPS))
                    flat = attn[:].rearrange("p h d -> p (h d)")
                    for k in range(KH):
                        last = nc.tensor.transpose(ps_attnT[:, k * T:(k + 1) * T], flat[:, k * P:(k + 1) * P],
                                                   id_sb[0:T, 0:T])
                    last.then_inc(attnT_ps, 1)
                elif step == "project":
                    pe.wait_ge(attnT_l, g + 1)
                    pe.wait_ge(xn_ready, min(g + 3, GROUPS))
                    if g >= 1:
                        pe.wait_ge(xn2_ready, g)
                    product(ps_proj, split(KH, (lambda k: attnT_hi[:, k], lambda k: attnT_lo[:, k]),
                                           (lambda k: proj_w[0][:, k], lambda k: proj_w[1][:, k]))
                            ).then_inc(proj_ps, 1)
                elif step == "ffn_t":
                    pe.wait_ge(xn2_ready, g + 1)
                    if g >= 1:
                        pe.wait_ge(x2_l, g)
                    pe.wait_ge(kT_ready, min(g + 2, GROUPS))
                    for k in range(KH):
                        last = nc.tensor.transpose(ps_x2T[:, k * T:(k + 1) * T], xn2[:, k * P:(k + 1) * P],
                                                   id_sb[0:T, 0:T])
                    last.then_inc(x2T_ps, 1)
                elif step == "logits":
                    pe.wait_ge(x2_l, g + 1)
                    if g >= 1:
                        pe.wait_ge(logit_ready, g)
                    pe.wait_ge(qkn_ready, min(g + 3, GROUPS))
                    at = slice(g * T, (g + 1) * T)
                    product(ps_logit, split(KH, (lambda k: x2_hi[:, k, at], lambda k: x2_lo[:, k, at]),
                                            (lambda k: gate_w[0][:, k], lambda k: gate_w[1][:, k]))
                            ).then_inc(logit_ps, 1)

            pe.wait_ge(coef_ready, 1)
            for g in range(GROUPS):
                if g >= 2:
                    pe.wait_ge(coefT_ready, g - 1)
                nc.tensor.transpose(banks[g % 2][0:EXPERTS, 0:T], coef[:, g], id_sb[0:T, 0:T]).then_inc(coefT_ps, 1)

            for c in range(2):
                for hid in range(KH):
                    first = True
                    for g in range(GROUPS):
                        lo, hi = max(g * T, c * HALF), min((g + 1) * T, (c + 1) * HALF)
                        if lo < hi:
                            nc.tensor.matmul(ps_y[c][hid][:, lo - c * HALF:hi - c * HALF],
                                             h_all[:, g, hid * P:(hid + 1) * P],
                                             id_sb[0:T, lo - g * T:hi - g * T], start=first, stop=False,
                                             skip_group_check=True)
                            first = False

            def down_product(u):
                e, unit = u // UNITS, u % UNITS
                c, m = unit // MT, unit % MT
                b = e % 2
                pe.wait_ge(mid_l, u + 1)
                for hid in range(KH):
                    for w, h in ((w_hi, mid_hi), (w_hi, mid_lo), (w_lo, mid_hi)):
                        last = nc.tensor.matmul(ps_y[c][hid], down(w[b], m, hid), h[:, u % HBUF], start=False,
                                                stop=False, skip_group_check=True)
                last.then_inc(downed, 1)

            pe.wait_ge(coefT_ready, GROUPS)
            for e in range(EXPERTS + 1):
                for unit in range(UNITS):
                    u = e * UNITS + unit
                    c, m = unit // MT, unit % MT
                    b = e % 2
                    chunk = slice(c * HALF, (c + 1) * HALF)
                    if unit == 0:
                        pe.wait_ge(we_lo, (e + 1) * PIECES)
                    if u >= 2:
                        pe.wait_ge(silu_ready, u - 1)
                        pe.wait_ge(mid_ready, u - 1)
                    for matrix, dst in ((0, ps_gate), (1, ps_up)):
                        last = product(dst[u % 2],
                                       split(KH, (lambda k: gate_up(w_hi[b], matrix, k, m),
                                                  lambda k: gate_up(w_lo[b], matrix, k, m)),
                                             (lambda k: x2_hi[:, k, chunk], lambda k: x2_lo[:, k, chunk])))
                    last.then_inc(gu_ps, 1)
                    if u >= LAG:
                        down_product(u - LAG)
            for u in range((EXPERTS + 1) * UNITS - LAG, (EXPERTS + 1) * UNITS):
                down_product(u)


def kernel(**inputs):
    import concourse.bacc as bacc
    from concourse.bass_utils import run_bass_kernel_spmd as run

    f = np.float32
    side = IMAGE // PATCH
    x = np.ascontiguousarray(inputs["x"])
    patches = x.reshape(BATCH, CHANNELS, side, PATCH, side, PATCH).transpose(0, 1, 3, 5, 2, 4)
    patches = patches.reshape(BATCH, PATCHES, FLAT).transpose(2, 0, 1)
    xt = np.zeros((FLAT, GROUPS * PER_GROUP, SEQ), f)
    xt[:, :BATCH, 1:] = patches
    xt = xt.reshape(KF, P, GROUPS, T).transpose(1, 2, 0, 3)
    clsrows = np.zeros((T, HID), f)
    clsrows[::SEQ] = inputs["cls_tok"][0, 0]

    def rows(w, k):
        return np.asarray(w).reshape(k, P, -1).transpose(1, 0, 2).reshape(P, -1)

    wq = np.asarray(inputs["L0_attn_Wq"]).reshape(KV, REP, D, HID).transpose(1, 0, 2, 3).reshape(HID, HID)
    wqkv = np.concatenate([wq, inputs["L0_attn_Wkv"]], 0).T
    wproj = np.asarray(inputs["L0_attn_Wproj"]).T.reshape(KV, REP, D, HID).transpose(1, 0, 2, 3).reshape(HID, HID)

    def expert(gate, up, dn):
        return np.concatenate([rows(gate, KH), rows(up, KH), rows(dn, MT)], 1)

    experts = np.stack([expert(inputs["L0_ffn_gate_proj_w"][e], inputs["L0_ffn_up_proj_w"][e],
                               inputs["L0_ffn_down_proj_w"][e]) for e in range(EXPERTS)])
    shared = expert(inputs["L0_ffn_shared_gate_w"][0], inputs["L0_ffn_shared_up_w"][0],
                    inputs["L0_ffn_shared_down_w"][0])
    theta = (1.0 / 10000.0 ** (np.arange(0, D, 2, dtype=f) / f(D))).astype(f)
    pos = np.tile(np.arange(SEQ, dtype=f), PER_GROUP)
    freqs = np.outer(pos, theta).astype(f)
    cos = np.concatenate([np.cos(freqs)] * 2, 1).astype(f)
    sin = np.concatenate([-np.sin(freqs), np.sin(freqs)], 1).astype(f)
    t = np.arange(T)
    mask = ((t[:, None] // SEQ == t[None] // SEQ) & (t[:, None] <= t[None])).astype(f)
    e = np.arange(EXPERTS)
    before = np.broadcast_to((e[None, :] < e[:, None]).astype(f), (T, EXPERTS, EXPERTS))

    arrays = {"x_in": xt, "cls_in": clsrows, "w_tok_in": rows(inputs["L0_tok_W"], KF), "w_qkv_in": rows(wqkv, KH),
              "w_proj_in": rows(wproj, KH), "w_gate_in": rows(np.asarray(inputs["L0_ffn_gate_w"]).T, KH),
              "beta_in": np.asarray(inputs["L0_ffn_beta"]), "w_exp_in": experts, "w_sh_in": shared, "cos_in": cos,
              "sin_in": sin, "mask_in": mask, "ident_in": np.eye(P, dtype=f), "before_in": before}
    arrays = {k: np.ascontiguousarray(v) for k, v in arrays.items()}
    nc = bacc.Bacc("TRN2", target_bir_lowering=False, num_devices=1)
    args = [nc.dram_tensor(k, v.shape, mybir.dt.from_np(v.dtype), kind="ExternalInput").ap()
            for k, v in arrays.items()]
    c_dram = nc.dram_tensor("coef_scratch", (EXPERTS, TOKENS), F32, kind="Internal").ap()
    out = nc.dram_tensor("out_dram", (HID, TOKENS), F32, kind="ExternalOutput").ap()
    vit_block(nc, *args, c_dram, out)
    r = run(nc, [arrays], core_ids=[0])
    got = r.results[0]["out_dram"]
    return np.ascontiguousarray(got.reshape(HID, BATCH, SEQ).transpose(1, 2, 0))
```

```python
from contextlib import ExitStack

import concourse.bass as bass
import numpy as np
from concourse import mybir

F32 = mybir.dt.float32
F32R = mybir.dt.float32r
ALU = mybir.AluOpType
ACT = mybir.ActivationFunctionType
AX_X = mybir.AxisListType.X

P = 128
BATCH, CHANNELS, IMAGE, PATCH = 16, 3, 96, 16
HID = 256
PATCHES = (IMAGE // PATCH) ** 2
SEQ = PATCHES + 1
TOKENS = BATCH * SEQ
FLAT = CHANNELS * PATCH * PATCH
KF = FLAT // P
KH = HID // P
PER_GROUP = P // SEQ
T = PER_GROUP * SEQ
GROUPS = -(-BATCH // PER_GROUP)
PADDED = GROUPS * T
HEADS, KV, D = 16, 4, 16
REP = HEADS // KV
QKV = HID + 2 * KV * D
WIDE = 2 * D
EXPERTS, MID = 8, 512
TOP = 2
MT = MID // P
LN_EPS = 1e-5
QK_EPS = 1e-6
SCALE = 1.0 / D ** 0.5
HALF = TOKENS // 2
EXPERT_COLS = 3 * KH * MID
PIECES = 6
PIECE = EXPERT_COLS // PIECES
UNITS = 2 * MT
COEF_UNIT = 4
LAG = 2
DEEP = 4
HBUF = 4


def schedule():
    order = [("split_x", 0), ("split_x", 1), ("embed_a", 0), ("embed_b", 0)]
    for i in range(-1, GROUPS + 2):
        order += [("qkv", i), ("heads_t", i - 2), ("embed_a", i + 2), ("qk_sum", i), ("ln_add", i + 1),
                  ("ln_stats", i + 1), ("qk_eps", i), ("ln_mean", i + 1), ("qk_inverse", i), ("qk_apply", i),
                  ("turn", i), ("split_x", i + 3), ("ln_apply", i + 1), ("norm_t", i + 1), ("embed_b", i + 2),
                  ("rotate", i - 1), ("stack", i - 1)]
    order += [("spread_k", 0)]
    pairs = GROUPS * KV
    for n in range(pairs + 2 * KV):
        if n < pairs:
            order += [("score", n)]
        if 0 <= n - 2 < pairs:
            order += [("value", n - 2)]
        g, j = n // KV, n % KV
        order += [("spread_k", g + 1)] * (j == 1 and n < pairs)
        order += [("out_t", g - 1)] * (j == 2) + [("attn_t", g - 1)] * (j == 3) + [("project", g - 2)] * (j == 1)
        if j == 2:
            order += [("split_w", g)]
    order += [("seed", 0), ("ln2_root", 0)]
    for i in range(GROUPS + 2):
        order += [("ln2_apply", i), ("ffn_t", i - 1), ("logits", i - 2)]
    limit = {"score": pairs, "value": pairs, "split_w": PIECES}
    return [(s, g) for s, g in order if 0 <= g < limit.get(s, GROUPS)]


def vit_block(nc, x, clsrows, w_tok, w_qkv, w_proj, w_gate, beta, w_exp, w_sh, rope, mask, ident,
              before, c_dram, out):
    with ExitStack() as ctx:
        def sb(name, shape, dt=F32):
            return ctx.enter_context(nc.sbuf_tensor(name, shape, dt))

        def sem(name):
            return ctx.enter_context(nc.semaphore(name))

        banks = [ctx.enter_context(nc.psum_tensor(f"bank{i}", [P, 512], F32)) for i in range(8)]

        early_late = sb("early_late", [P, max(GROUPS * KF * T, EXPERTS * TOKENS)])
        xraw = early_late[:, 0:GROUPS * KF * T].rearrange("p (g k t) -> p g k t", g=GROUPS, k=KF)
        split_hi = [sb(f"split_hi{i}", [P, KF * T], F32R) for i in range(2)]
        split_lo = [sb(f"split_lo{i}", [P, KF * T], F32R) for i in range(2)]
        x_hi = [t[:].rearrange("p (k t) -> p k t", k=KF) for t in split_hi]
        x_lo = [t[:].rearrange("p (k t) -> p k t", k=KF) for t in split_lo]
        small_raw = sb("small_raw", [P, KF * HID + KH * (QKV + HID + EXPERTS)])
        small_hi = sb("small_hi", [P, KF * HID + KH * (QKV + HID + EXPERTS)], F32R)
        small_lo = sb("small_lo", [P, KF * HID + KH * (QKV + HID + EXPERTS)], F32R)
        cls_sb = sb("cls_sb", [T, HID])
        beta_sb = sb("beta_sb", [T, EXPERTS])
        rope_sb = sb("rope_sb", [T, 2 * D])
        cos_sb, sin_sb = rope_sb[:, 0:D], rope_sb[:, D:2 * D]
        mask_sb = sb("mask_sb", [T, T])
        id_sb = sb("id_sb", [P, P])
        before_sb = sb("before_sb", [T, EXPERTS, EXPERTS])

        def weights(t, at, k, n):
            return t[:, at:at + k * n].rearrange("p (k n) -> p k n", k=k)

        at_qkv = KF * HID
        at_proj = at_qkv + KH * QKV
        at_gate = at_proj + KH * HID
        tok_w = [weights(t, 0, KF, HID) for t in (small_hi, small_lo)]
        qkv_w = [weights(t, at_qkv, KH, QKV) for t in (small_hi, small_lo)]
        proj_w = [weights(t, at_proj, KH, HID) for t in (small_hi, small_lo)]
        gate_w = [weights(t, at_gate, KH, EXPERTS) for t in (small_hi, small_lo)]

        h_all = sb("h_all", [T, GROUPS, HID])
        stats = sb("stats", [T, 2, GROUPS, 6])
        moments = sb("moments", [T, 2, GROUPS, 2])
        deviation = sb("deviation", [T, 2, GROUPS])
        rstd = sb("rstd", [T, 2, GROUPS])
        ln_eps = sb("ln_eps", [T, 1])
        xn = sb("xn", [T, HID])
        xnT_hi = sb("xnT_hi", [P, KH, T], F32R)
        xnT_lo = sb("xnT_lo", [P, KH, T], F32R)
        squares = sb("squares", [T, HEADS + KV, D])
        norm2 = sb("norm2", [T, HEADS + KV])
        root = sb("root", [T, HEADS + KV])
        norm = sb("norm", [T, HEADS + KV])
        inv_norm = sb("inv_norm", [T, HEADS + KV])
        qkn = sb("qkn", [T, HEADS + KV, D])
        turned = [sb(f"turned{i}", [T, HEADS + KV, D]) for i in range(2)]
        rot = [sb(f"rot{i}", [T, HEADS + KV, D]) for i in range(2)]
        heads = sb("heads", [T, HEADS + 2 * KV, WIDE])
        v_one = sb("v_one", [T, GROUPS, KV, WIDE])
        kT = [sb(f"kT{g}", [P, 2, T], F32R) for g in range(GROUPS)]
        k_own = [sb(f"k_own{i}", [P, KV, 2, T], F32R) for i in range(2)]
        attn_ffn = [sb(f"attn_ffn{i}", [P, REP * T]) for i in range(DEEP)]
        probs = [t[0:T].rearrange("p (r t) -> p r t", r=REP) for t in attn_ffn]
        oT = sb("oT", [P, REP * T])
        inv_den = sb("inv_den", [T, HEADS])
        attn = sb("attn", [T, HEADS, D])
        attnT_hi = sb("attnT_hi", [P, KH, T], F32R)
        attnT_lo = sb("attnT_lo", [P, KH, T], F32R)
        xn2 = [sb(f"xn2{i}", [T, HID]) for i in range(2)]
        x2_hi = sb("x2_hi", [P, KH, PADDED], F32R)
        x2_lo = sb("x2_lo", [P, KH, PADDED], F32R)
        logits = sb("logits", [T, GROUPS, EXPERTS])
        biased = sb("biased", [T, GROUPS, EXPERTS])

        greater = sb("greater", [T, GROUPS, EXPERTS * EXPERTS])
        equal = sb("equal", [T, GROUPS, EXPERTS * EXPERTS])
        rank = sb("rank", [T, GROUPS, EXPERTS])
        expneg = sb("expneg", [T, GROUPS, EXPERTS])
        sigm = sb("sigm", [T, GROUPS, EXPERTS])
        coef = sb("coef", [T, GROUPS, EXPERTS])
        coefT = sb("coefT", [EXPERTS, PADDED])
        cbc = early_late[:, 0:EXPERTS * TOKENS].rearrange("p (e t) -> p e t", e=EXPERTS)

        wraw = [sb(f"wraw{i}", [P, EXPERT_COLS]) for i in range(2)]
        w_hi = [sb(f"w_hi{i}", [P, EXPERT_COLS], F32R) for i in range(2)]
        w_lo = [sb(f"w_lo{i}", [P, EXPERT_COLS], F32R) for i in range(2)]
        qT = [w_lo[1][:, g * REP * T:(g + 1) * REP * T] for g in range(GROUPS)]
        silu = [attn_ffn[i][:, 0:HALF] for i in range(2)]
        upc = [attn_ffn[2 + i][:, 0:HALF] for i in range(2)]
        mid = [sb(f"mid{i}", [P, HALF]) for i in range(2)]
        mid_hi, mid_lo = ([t[:, i * HALF:(i + 1) * HALF] for t in two for i in range(2)]
                          for two in (split_hi, split_lo))
        result = small_raw[:, 0:KH * TOKENS].rearrange("p (k t) -> p k t", k=KH)

        def gate_up(t, matrix, k, m):
            at = (matrix * KH + k) * MID + m * P
            return t[:, at:at + P]

        def down(t, m, hid):
            at = 2 * KH * MID + m * HID + hid * P
            return t[:, at:at + P]

        ps_embed = [banks[0][0:T, 0:HID], banks[1][0:T, 0:HID]]
        ps_xnT = banks[2][:, 0:KH * T]
        ps_qkv = [banks[3][0:T, 0:QKV], banks[4][0:T, 0:QKV]]
        ps_qT = banks[5][:, 0:REP * T]
        ps_kT = banks[6][:, 0:2 * T]
        ps_score = [banks[i][0:T, 0:REP * T] for i in range(DEEP)]
        ps_value = [banks[4][:, 0:REP * T], banks[5][:, 0:REP * T]]
        ps_out = banks[6][0:T, :]
        ps_attnT = banks[7][:, 0:KH * T]
        ps_proj = banks[7][0:T, 256:256 + HID]
        ps_x2T = [banks[0][:, 0:KH * T], banks[1][:, 0:KH * T]]
        ps_logit = banks[2][0:T, 0:GROUPS * EXPERTS].rearrange("p (g e) -> p g e", e=EXPERTS)
        ps_gate = [banks[0][:, 0:HALF], banks[1][:, 0:HALF]]
        ps_up = [banks[2][:, 0:HALF], banks[3][:, 0:HALF]]
        ps_y = [[banks[4 + 2 * c + hid][:, 0:HALF] for hid in range(KH)] for c in range(2)]

        d_x = [sem(f"d_x{g}") for g in range(GROUPS)]
        d_tok = sem("d_tok")
        d_small = sem("d_small")
        d_cls = sem("d_cls")
        d_id = sem("d_id")
        d_rope = sem("d_rope")
        d_mask = sem("d_mask")
        d_late = sem("d_late")
        d_shared = sem("d_shared")
        d_expert = [sem("d_expert0"), sem("d_expert1")]
        d_coef = sem("d_coef")
        d_cbc = sem("d_cbc")
        d_out = sem("d_out")

        ws_hi = sem("ws_hi")
        ws_lo = sem("ws_lo")
        fill = sem("fill")
        xs_hi = sem("xs_hi")
        xs_lo = sem("xs_lo")
        embedded = sem("embedded")
        h_ready = sem("h_ready")
        xn_ready = sem("xn_ready")
        ln1_stats = sem("ln1_stats")
        ln2_stats = sem("ln2_stats")
        ln1_root = sem("ln1_root")
        ln2_root = sem("ln2_root")
        norm2_ready = sem("norm2_ready")
        root_ready = sem("root_ready")
        xnT_ps = sem("xnT_ps")
        xnT_h = sem("xnT_h")
        xnT_l = sem("xnT_l")
        qkv_ps = sem("qkv_ps")
        sq_ready = sem("sq_ready")
        v_ready = sem("v_ready")
        qkn_ready = sem("qkn_ready")
        turned_ready = sem("turned_ready")
        rot_ready = sem("rot_ready")
        heads_h = sem("heads_h")
        heads_l = sem("heads_l")
        heads_ps = sem("heads_ps")
        zeroed = sem("zeroed")
        k_ready = sem("k_ready")
        qT_ready = sem("qT_ready")
        kT_ready = sem("kT_ready")
        score_ps = sem("score_ps")
        exp_ready = sem("exp_ready")
        prob_ready = [sem("prob_ready0"), sem("prob_ready1")]
        value_ps = sem("value_ps")
        oT_ready = sem("oT_ready")
        out_ps = sem("out_ps")
        attn_ready = sem("attn_ready")
        attnT_ps = sem("attnT_ps")
        attnT_h = sem("attnT_h")
        attnT_l = sem("attnT_l")
        proj_ps = sem("proj_ps")
        h2_ready = sem("h2_ready")
        xn2_ready = sem("xn2_ready")
        x2T_ps = sem("x2T_ps")
        x2_h = sem("x2_h")
        x2_l = sem("x2_l")
        logit_ps = sem("logit_ps")
        logit_ready = sem("logit_ready")
        expneg_ready = sem("expneg_ready")
        coef_ready = sem("coef_ready")
        coefT_ps = sem("coefT_ps")
        coefT_ready = sem("coefT_ready")
        dve_step = sem("dve_step")
        we_hi = sem("we_hi")
        we_lo = sem("we_lo")
        gu_ps = sem("gu_ps")
        silu_ready = sem("silu_ready")
        up_read = sem("up_read")
        mid_ready = sem("mid_ready")
        mid_h = sem("mid_h")
        mid_l = sem("mid_l")
        downed = sem("downed")
        y_ready = sem("y_ready")

        block = ctx.enter_context(nc.Block())
        ORDER = schedule()

        @block.sync
        def _(sp):
            n_tok = KF * HID
            sp.dma_start(xraw[:, 0], x[:, 0]).then_inc(d_x[0], 16)
            sp.dma_start(small_raw[:, 0:n_tok], w_tok).then_inc(d_tok, 16)
            sp.dma_start(cls_sb[:], clsrows).then_inc(d_cls, 16)
            sp.dma_start(id_sb[:], ident).then_inc(d_id, 16)
            sp.dma_start(small_raw[:, at_qkv:at_proj], w_qkv).then_inc(d_small, 16)
            for g in range(1, GROUPS):
                sp.dma_start(xraw[:, g], x[:, g]).then_inc(d_x[g], 16)
                if g == 1:
                    sp.dma_start(rope_sb[:], rope).then_inc(d_rope, 16)
                    sp.dma_start(mask_sb[:], mask).then_inc(d_mask, 16)
                    sp.dma_start(small_raw[:, at_proj:at_gate], w_proj).then_inc(d_small, 16)
                    sp.dma_start(small_raw[:, at_gate:], w_gate).then_inc(d_small, 16)
            sp.dma_start(wraw[0][:], w_sh).then_inc(d_shared, 16)
            sp.dma_start(wraw[1][:], w_exp[0]).then_inc(d_expert[0], 16)
            sp.wait_ge(coefT_ready, 2)
            sp.dma_start(c_dram, coefT[:, 0:TOKENS]).then_inc(d_coef, 16)
            sp.wait_ge(d_coef, 16)
            sp.dma_start(cbc, c_dram.partition_broadcast(P)).then_inc(d_cbc, 16)
            for e in range(1, EXPERTS):
                sp.wait_ge(we_lo, PIECES * e)
                sp.dma_start(wraw[(e + 1) % 2][:], w_exp[e]).then_inc(d_expert[e % 2], 16)
            for hid in range(KH):
                sp.wait_ge(y_ready, 2 * hid + 2)
                sp.dma_start(out[hid * P:(hid + 1) * P, :], result[:, hid]).then_inc(d_out, 16)
            sp.wait_ge(d_out, 16 * KH)

        @block.gpsimd
        def _(pool):
            for i in range(2):
                pool.memset(k_own[i][:].bitcast(mybir.dt.uint32), 0).then_inc(zeroed, 1)
            pool.dma_start(before_sb[:], before).then_inc(d_late, 16)
            pool.dma_start(beta_sb[:], beta.partition_broadcast(T)).then_inc(d_late, 16)
            for step, g in ORDER:
                if step == "split_x":
                    pool.wait_ge(xs_hi, g + 1)
                    if g >= 2:
                        pool.wait_ge(embedded, g - 1)
                    nc.gpsimd.tensor_tensor(x_lo[g % 2], xraw[:, g], x_hi[g % 2].bitcast(F32),
                                            ALU.subtract).then_inc(xs_lo, 1)
                elif step == "turn":
                    if g == 0:
                        pool.wait_ge(d_rope, 16)
                    pool.wait_ge(qkn_ready, g + 1)
                    if g >= 2:
                        pool.wait_ge(heads_l, g - 1)
                    nc.gpsimd.tensor_tensor(rot[g % 2][:], qkn[:], cos_sb[:, None, :].broadcast_to([T, HEADS + KV, D]),
                                            ALU.mult)
                    nc.gpsimd.tensor_tensor(
                        turned[g % 2][:, :, 0:D // 2], qkn[:, :, D // 2:D],
                        sin_sb[:, None, 0:D // 2].broadcast_to([T, HEADS + KV, D // 2]), ALU.mult)
                    nc.gpsimd.tensor_tensor(
                        turned[g % 2][:, :, D // 2:D], qkn[:, :, 0:D // 2],
                        sin_sb[:, None, D // 2:D].broadcast_to([T, HEADS + KV, D // 2]),
                        ALU.mult).then_inc(turned_ready, 1)
                elif step == "score" and g % 2 == 0:
                    if g == 0:
                        pool.wait_ge(d_mask, 16)
                    pool.wait_ge(exp_ready, g + 1)
                    nc.gpsimd.tensor_tensor(probs[g % DEEP], probs[g % DEEP],
                                            mask_sb[:, None, :].broadcast_to([T, REP, T]),
                                            ALU.mult).then_inc(prob_ready[0], 1)

        @block.scalar
        def _(act):
            def copy(dst, src):
                return nc.scalar.activation(dst, src, ACT.Copy)

            act.wait_ge(d_tok, 16)
            copy(small_hi[:, 0:at_qkv], small_raw[:, 0:at_qkv]).then_inc(ws_hi, 1)

            def weights_hi(e, piece):
                at = slice(piece * PIECE, (piece + 1) * PIECE)
                b = e % 2
                copy(w_hi[b][:, at], wraw[b][:, at]).then_inc(we_hi, 1)

            for step, g in ORDER:
                if step == "split_x":
                    act.wait_ge(d_x[g], 16)
                    if g >= 2:
                        act.wait_ge(embedded, g - 1)
                    copy(x_hi[g % 2], xraw[:, g]).then_inc(xs_hi, 1)
                    if g == 1:
                        act.wait_ge(d_small, 48)
                        copy(small_hi[:, at_qkv:], small_raw[:, at_qkv:]).then_inc(ws_hi, 1)
                elif step == "norm_t":
                    act.wait_ge(xnT_ps, g + 1)
                    if g >= 1:
                        act.wait_ge(qkv_ps, g)
                    copy(xnT_hi[:].rearrange("p k t -> p (k t)"), ps_xnT).then_inc(xnT_h, 1)
                elif step == "ln_mean":
                    if g == 0:
                        act.wait_ge(fill, 2)
                    act.wait_ge(ln1_stats, g + 1)
                    nc.scalar.activation(deviation[:, 0, g:g + 1], moments[:, 0, g, 1:2], ACT.Sqrt,
                                         bias=ln_eps[:, 0:1]).then_inc(ln1_root, 1)
                elif step == "qkv":
                    act.wait_ge(qkv_ps, g + 1)
                    if g >= 1:
                        act.wait_ge(norm2_ready, g)
                    nc.scalar.activation(squares[:].rearrange("p h d -> p (h d)"),
                                         ps_qkv[g % 2][:, 0:HID + KV * D], ACT.Square).then_inc(sq_ready, 1)
                    copy(v_one[:, g, :, 0:D], ps_qkv[g % 2][:, HID + KV * D:QKV].rearrange(
                        "p (j d) -> p j d", j=KV)).then_inc(v_ready, 1)
                elif step == "qk_sum":
                    act.wait_ge(norm2_ready, g + 1)
                    nc.scalar.activation(root[:], norm2[:], ACT.Sqrt).then_inc(root_ready, 1)
                elif step == "stack":
                    act.wait_ge(rot_ready, g + 1)
                    if g >= 1:
                        act.wait_ge(heads_ps, g)
                    hr = heads[:].bitcast(F32R)
                    copy(hr[:, 0:HEADS, 0:D], rot[g % 2][:, 0:HEADS])
                    k4 = hr[:, HEADS:HEADS + KV].rearrange("p j (two d) -> p j two d", two=2)
                    copy(k4, rot[g % 2][:, HEADS:HEADS + KV, None, :].broadcast_to([T, KV, 2, D])).then_inc(heads_h, 1)
                elif step == "heads_t":
                    act.wait_ge(heads_ps, g + 1)
                    copy(qT[g], ps_qT).then_inc(qT_ready, 1)
                    copy(kT[g][:].rearrange("p k t -> p (k t)"), ps_kT).then_inc(kT_ready, 1)
                elif step == "score":
                    act.wait_ge(score_ps, g + 1)
                    if g >= DEEP:
                        act.wait_ge(value_ps, g - DEEP + 1)
                    nc.scalar.activation(probs[g % DEEP].rearrange("p r t -> p (r t)"), ps_score[g % DEEP],
                                         ACT.Exp, scale=SCALE).then_inc(exp_ready, 1)
                elif step == "out_t":
                    act.wait_ge(value_ps, KV * (g + 1))
                    if g >= 1:
                        act.wait_ge(out_ps, g)
                    copy(oT[:], ps_value[g % 2]).then_inc(oT_ready, 1)
                elif step == "attn_t":
                    act.wait_ge(attnT_ps, g + 1)
                    if g >= 1:
                        act.wait_ge(proj_ps, g)
                    copy(attnT_hi[:].rearrange("p k t -> p (k t)"), ps_attnT).then_inc(attnT_h, 1)
                elif step == "split_w":
                    act.wait_ge(d_shared, 16)
                    weights_hi(0, g)
                elif step == "ln2_root":
                    act.wait_ge(ln2_stats, GROUPS)
                    nc.scalar.activation(deviation[:, 1], moments[:, 1, :, 1], ACT.Sqrt,
                                         bias=ln_eps[:, 0:1]).then_inc(ln2_root, 1)
                elif step == "ffn_t":
                    act.wait_ge(x2T_ps, g + 1)
                    copy(x2_hi[:, :, g * T:(g + 1) * T],
                         ps_x2T[g % 2].rearrange("p (k t) -> p k t", k=KH)).then_inc(x2_h, 1)
            act.wait_ge(logit_ready, 1)
            nc.scalar.activation(expneg[:], logits[:], ACT.Exp, scale=-1.0).then_inc(expneg_ready, 1)

            for e in range(EXPERTS + 1):
                for unit in range(UNITS):
                    u = e * UNITS + unit
                    act.wait_ge(gu_ps, u + 1)
                    if u >= 2:
                        act.wait_ge(mid_ready, u - 1)
                    nc.scalar.activation(silu[u % 2], ps_gate[u % 2], ACT.Silu).then_inc(silu_ready, 1)
                    if e < EXPERTS and unit >= LAG:
                        piece = unit - LAG
                        if piece == 0:
                            act.wait_ge(d_expert[e % 2], 16 * (e // 2 + 1))
                            act.wait_ge(downed, u - LAG)
                        weights_hi(e + 1, piece)
                    act.wait_ge(mid_ready, u + 1)
                    if u >= HBUF:
                        act.wait_ge(downed, u - HBUF + 1)
                    copy(mid_hi[u % HBUF], mid[u % 2][:]).then_inc(mid_h, 1)

        @block.vector
        def _(dve):
            steps = [0]
            mark = {}

            def note(ins, what, g):
                steps[0] += 1
                ins.then_inc(dve_step, 1)
                mark[what, g] = steps[0]

            def after(what, g):
                dve.wait_ge(dve_step, mark[what, g])

            def settle(ins):
                steps[0] += 1
                ins.then_inc(dve_step, 1)
                dve.wait_ge(dve_step, steps[0])

            def statistics(g, which, ready):
                settle(nc.vector.bn_stats(stats[:, which, g], h_all[:, g]))
                nc.vector.bn_aggr(moments[:, which, g], stats[:, which, g]).then_inc(ready, 1)

            def normalize(g, which, dst, ready):
                nc.vector.tensor_scalar(dst, h_all[:, g], moments[:, which, g, 0:1], rstd[:, which, g:g + 1],
                                        ALU.subtract, ALU.mult).then_inc(ready, 1)

            def weights_lo(e, piece):
                at = slice(piece * PIECE, (piece + 1) * PIECE)
                b = e % 2
                dve.wait_ge(we_hi, e * PIECES + piece + 1)
                nc.vector.tensor_tensor(w_lo[b][:, at], wraw[b][:, at], w_hi[b][:, at].bitcast(F32),
                                        ALU.subtract).then_inc(we_lo, 1)

            settle(nc.vector.memset(v_one[:, :, :, D:WIDE], 0.0))
            nc.vector.memset(v_one[:, :, :, D:D + 1], 1.0).then_inc(fill, 1)
            nc.vector.memset(ln_eps[:], LN_EPS).then_inc(fill, 1)
            dve.wait_ge(ws_hi, 1)
            nc.vector.tensor_tensor(small_lo[:, 0:at_qkv], small_raw[:, 0:at_qkv],
                                    small_hi[:, 0:at_qkv].bitcast(F32), ALU.subtract).then_inc(ws_lo, 1)
            for step, g in ORDER:
                if step == "split_x" and g == 1:
                    dve.wait_ge(ws_hi, 2)
                    nc.vector.tensor_tensor(small_lo[:, at_qkv:], small_raw[:, at_qkv:],
                                            small_hi[:, at_qkv:].bitcast(F32), ALU.subtract).then_inc(ws_lo, 1)
                elif step == "ln_add":
                    if g == 0:
                        dve.wait_ge(d_cls, 16)
                    dve.wait_ge(embedded, g + 1)
                    nc.vector.tensor_tensor(h_all[:, g], ps_embed[g % 2], cls_sb[:], ALU.add).then_inc(h_ready, 1)
                elif step == "ln_stats":
                    dve.wait_ge(h_ready, g + 1)
                    note(nc.vector.bn_stats(stats[:, 0, g], h_all[:, g]), step, g)
                elif step == "ln_mean":
                    after("ln_stats", g)
                    nc.vector.bn_aggr(moments[:, 0, g], stats[:, 0, g]).then_inc(ln1_stats, 1)
                elif step == "ln_apply":
                    dve.wait_ge(ln1_root, g + 1)
                    note(nc.vector.reciprocal(rstd[:, 0, g:g + 1], deviation[:, 0, g:g + 1]), step, g)
                    if g >= 1:
                        dve.wait_ge(xnT_ps, g)
                    after("ln_apply", g)
                    normalize(g, 0, xn[:], xn_ready)
                elif step == "norm_t":
                    dve.wait_ge(xnT_h, g + 1)
                    nc.vector.tensor_tensor(xnT_lo[:].rearrange("p k t -> p (k t)"), ps_xnT,
                                            xnT_hi[:].rearrange("p k t -> p (k t)").bitcast(F32),
                                            ALU.subtract).then_inc(xnT_l, 1)
                elif step == "qk_sum":
                    dve.wait_ge(sq_ready, g + 1)
                    nc.vector.reduce_sum(norm2[:], squares[:], AX_X).then_inc(norm2_ready, 1)
                elif step == "qk_eps":
                    dve.wait_ge(root_ready, g + 1)
                    note(nc.vector.tensor_scalar(norm[:], root[:], QK_EPS, None, ALU.add), step, g)
                elif step == "qk_inverse":
                    after("qk_eps", g)
                    note(nc.vector.reciprocal(inv_norm[:], norm[:]), step, g)
                elif step == "qk_apply":
                    after("qk_inverse", g)
                    if g >= 1:
                        dve.wait_ge(turned_ready, g)
                    dve.wait_ge(v_ready, g + 1)
                    nc.vector.tensor_tensor(
                        qkn[:], ps_qkv[g % 2][:, 0:HID + KV * D].rearrange("p (h d) -> p h d", d=D),
                        inv_norm[:, :, None].broadcast_to([T, HEADS + KV, D]), ALU.mult).then_inc(qkn_ready, 1)
                elif step == "rotate":
                    dve.wait_ge(turned_ready, g + 1)
                    nc.vector.tensor_tensor(rot[g % 2][:], rot[g % 2][:], turned[g % 2][:], ALU.add).then_inc(rot_ready, 1)
                elif step == "stack":
                    dve.wait_ge(heads_h, g + 1)
                    nc.vector.tensor_tensor(heads[:, 0:HEADS, D:WIDE], rot[g % 2][:, 0:HEADS], heads[:, 0:HEADS, 0:D],
                                            ALU.subtract)
                    k4 = heads[:, HEADS + KV:].rearrange("p j (two d) -> p j two d", two=2)
                    h4 = heads[:, HEADS:HEADS + KV].rearrange("p j (two d) -> p j two d", two=2)
                    nc.vector.tensor_tensor(k4, rot[g % 2][:, HEADS:HEADS + KV, None, :].broadcast_to([T, KV, 2, D]),
                                            h4, ALU.subtract).then_inc(heads_l, 1)
                elif step == "spread_k":
                    dve.wait_ge(kT_ready, g + 1)
                    if g == 0:
                        dve.wait_ge(zeroed, 2)
                    if g >= 2:
                        dve.wait_ge(score_ps, KV * (g - 1))
                    for j in range(KV):
                        rows = slice(WIDE * j, WIDE * (j + 1))
                        last = nc.vector.tensor_copy(k_own[g % 2][rows, j], kT[g][rows])
                    last.then_inc(k_ready, 1)
                elif step == "score" and g % 2 == 1:
                    if g == 1:
                        dve.wait_ge(d_mask, 16)
                    dve.wait_ge(exp_ready, g + 1)
                    nc.vector.tensor_tensor(probs[g % DEEP], probs[g % DEEP],
                                            mask_sb[:, None, :].broadcast_to([T, REP, T]),
                                            ALU.mult).then_inc(prob_ready[1], 1)
                elif step == "out_t":
                    dve.wait_ge(out_ps, g + 1)
                    o4 = ps_out.rearrange("p (h w) -> p h w", w=WIDE)
                    settle(nc.vector.reciprocal(inv_den[:, :, None], o4[:, :, D:D + 1]))
                    if g >= 1:
                        dve.wait_ge(attnT_ps, g)
                    nc.vector.tensor_tensor(attn[:], o4[:, :, 0:D],
                                            inv_den[:, :, None].broadcast_to([T, HEADS, D]),
                                            ALU.mult).then_inc(attn_ready, 1)
                elif step == "attn_t":
                    dve.wait_ge(attnT_h, g + 1)
                    nc.vector.tensor_tensor(attnT_lo[:].rearrange("p k t -> p (k t)"), ps_attnT,
                                            attnT_hi[:].rearrange("p k t -> p (k t)").bitcast(F32),
                                            ALU.subtract).then_inc(attnT_l, 1)
                elif step == "project":
                    dve.wait_ge(proj_ps, g + 1)
                    nc.vector.tensor_tensor(h_all[:, g], h_all[:, g], ps_proj, ALU.add).then_inc(h2_ready, 1)
                    dve.wait_ge(h2_ready, g + 1)
                    statistics(g, 1, ln2_stats)
                elif step == "split_w":
                    weights_lo(0, g)
                elif step == "ln2_root":
                    dve.wait_ge(ln2_root, 1)
                    settle(nc.vector.reciprocal(rstd[:, 1], deviation[:, 1]))
                elif step == "ln2_apply":
                    if g >= 2:
                        dve.wait_ge(x2T_ps, g - 1)
                    normalize(g, 1, xn2[g % 2][:], xn2_ready)
                elif step == "ffn_t":
                    dve.wait_ge(x2_h, g + 1)
                    at = slice(g * T, (g + 1) * T)
                    nc.vector.tensor_tensor(x2_lo[:, :, at], ps_x2T[g % 2].rearrange("p (k t) -> p k t", k=KH),
                                            x2_hi[:, :, at].bitcast(F32), ALU.subtract).then_inc(x2_l, 1)

            dve.wait_ge(d_late, 32)
            dve.wait_ge(logit_ps, GROUPS)
            nc.vector.tensor_copy(logits[:], ps_logit).then_inc(logit_ready, 1)
            nc.vector.tensor_tensor(biased[:], ps_logit, beta_sb[:, None, :].broadcast_to([T, GROUPS, EXPERTS]),
                                    ALU.add).then_inc(logit_ready, 1)
            dve.wait_ge(logit_ready, 2)
            for g in range(GROUPS):
                shape = [T, EXPERTS, EXPERTS]
                mine = biased[:, g, :, None].broadcast_to(shape)
                other = biased[:, g, None, :].broadcast_to(shape)
                gr = greater[:, g].rearrange("p (e f) -> p e f", f=EXPERTS)
                eq = equal[:, g].rearrange("p (e f) -> p e f", f=EXPERTS)
                nc.vector.tensor_tensor(gr, other, mine, ALU.is_gt)
                nc.vector.tensor_tensor(eq, other, mine, ALU.is_equal).then_inc(dve_step, 1)
                steps[0] += 1
            dve.wait_ge(dve_step, steps[0])
            settle(nc.vector.tensor_tensor(
                equal[:], equal[:], before_sb[:].rearrange("p e f -> p (e f)")[:, None, :].broadcast_to(
                    [T, GROUPS, EXPERTS * EXPERTS]), ALU.mult))
            settle(nc.vector.tensor_tensor(greater[:], greater[:], equal[:], ALU.add))
            settle(nc.vector.reduce_sum(rank[:], greater[:].rearrange("p g (e f) -> p g e f", f=EXPERTS), AX_X))
            dve.wait_ge(expneg_ready, 1)
            settle(nc.vector.tensor_scalar(expneg[:], expneg[:], 1.0, None, ALU.add))
            settle(nc.vector.reciprocal(sigm[:], expneg[:]))
            nc.vector.scalar_tensor_tensor(coef[:], rank[:], TOP - 0.5, sigm[:], ALU.is_lt,
                                           ALU.mult).then_inc(coef_ready, 1)
            for e in range(EXPERTS + 1):
                for unit in range(UNITS):
                    u = e * UNITS + unit
                    chunk = slice((unit // MT) * HALF, (unit // MT + 1) * HALF)
                    if u == COEF_UNIT:
                        dve.wait_ge(coefT_ps, 1)
                        for half in range(2):
                            nc.vector.tensor_copy(coefT[:, half * 3 * T:(half + 1) * 3 * T],
                                                  banks[half][0:EXPERTS, 0:3 * T]).then_inc(coefT_ready, 1)
                    dve.wait_ge(gu_ps, u + 1)
                    if e == 0:
                        dve.wait_ge(silu_ready, u + 1)
                        if u >= 2:
                            dve.wait_ge(mid_h, u - 1)
                        nc.vector.tensor_tensor(mid[u % 2][:], ps_up[u % 2], silu[u % 2],
                                                ALU.mult).then_inc(mid_ready, 1)
                    else:
                        if u == UNITS:
                            dve.wait_ge(d_cbc, 16)
                        nc.vector.tensor_tensor(upc[u % 2], ps_up[u % 2], cbc[:, e - 1, chunk],
                                                ALU.mult).then_inc(up_read, 1)
                        dve.wait_ge(silu_ready, u + 1)
                        dve.wait_ge(up_read, u - UNITS + 1)
                        dve.wait_ge(mid_h, u - 1)
                        nc.vector.tensor_tensor(mid[u % 2][:], upc[u % 2], silu[u % 2],
                                                ALU.mult).then_inc(mid_ready, 1)
                    if e < EXPERTS and unit >= LAG:
                        weights_lo(e + 1, unit - LAG)
                    dve.wait_ge(mid_h, u + 1)
                    nc.vector.tensor_tensor(mid_lo[u % HBUF], mid[u % 2][:], mid_hi[u % HBUF].bitcast(F32),
                                            ALU.subtract).then_inc(mid_l, 1)
            dve.wait_ge(downed, (EXPERTS + 1) * UNITS)
            for hid in range(KH):
                for c in range(2):
                    nc.vector.tensor_copy(result[:, hid, c * HALF:(c + 1) * HALF], ps_y[c][hid]).then_inc(y_ready, 1)

        @block.tensor
        def _(pe):
            def product(dst, pairs):
                for i, (left, right) in enumerate(pairs):
                    last = nc.tensor.matmul(dst, left, right, start=(i == 0), stop=(i == len(pairs) - 1))
                return last

            def split(chunks, left, right):
                return [(left[a](k), right[b](k)) for k in range(chunks) for a, b in ((0, 0), (0, 1), (1, 0))]

            def embed_pairs(g):
                xh, xl = x_hi[g % 2], x_lo[g % 2]
                return split(KF, (lambda k: xh[:, k], lambda k: xl[:, k]),
                             (lambda k: tok_w[0][:, k], lambda k: tok_w[1][:, k]))

            pe.wait_ge(d_id, 16)
            for step, g in ORDER:
                if step == "embed_a":
                    if g == 0:
                        pe.wait_ge(ws_lo, 1)
                    if g >= 2:
                        pe.wait_ge(h_ready, g - 1)
                    pe.wait_ge(xs_lo, g + 1)
                    for n, (left, right) in enumerate(embed_pairs(g)[:3 * KF // 2]):
                        nc.tensor.matmul(ps_embed[g % 2], left, right, start=(n == 0), stop=False,
                                         skip_group_check=True)
                elif step == "embed_b":
                    rest = embed_pairs(g)[3 * KF // 2:]
                    for n, (left, right) in enumerate(rest):
                        last = nc.tensor.matmul(ps_embed[g % 2], left, right, start=False,
                                                stop=(n == len(rest) - 1), skip_group_check=True)
                    last.then_inc(embedded, 1)
                elif step == "norm_t":
                    pe.wait_ge(xn_ready, g + 1)
                    if g >= 1:
                        pe.wait_ge(xnT_l, g)
                    for k in range(KH):
                        last = nc.tensor.transpose(ps_xnT[:, k * T:(k + 1) * T], xn[:, k * P:(k + 1) * P],
                                                   id_sb[0:T, 0:T])
                    last.then_inc(xnT_ps, 1)
                elif step == "qkv":
                    if g == 0:
                        pe.wait_ge(ws_lo, 2)
                    if g >= 2:
                        pe.wait_ge(qkn_ready, g - 1)
                    pe.wait_ge(xnT_l, g + 1)
                    product(ps_qkv[g % 2], split(KH, (lambda k: xnT_hi[:, k], lambda k: xnT_lo[:, k]),
                                                 (lambda k: qkv_w[0][:, k], lambda k: qkv_w[1][:, k]))
                            ).then_inc(qkv_ps, 1)
                elif step == "heads_t":
                    pe.wait_ge(heads_l, g + 1)
                    if g >= 1:
                        pe.wait_ge(qT_ready, g)
                        pe.wait_ge(kT_ready, g)
                    blocks = heads[:].rearrange("p (b j) w -> p b (j w)", j=KV)
                    for b in range(REP + 2):
                        dst = ps_qT if b < REP else ps_kT
                        at = (b % REP) * T
                        last = nc.tensor.transpose(dst[:, at:at + T], blocks[:, b], id_sb[0:T, 0:T])
                    last.then_inc(heads_ps, 1)
                elif step == "score":
                    if g == 0:
                        pe.wait_ge(h_ready, GROUPS)
                    if g == 2:
                        pe.wait_ge(xnT_l, GROUPS)
                    if g == 3:
                        pe.wait_ge(qkn_ready, GROUPS)
                    if g % KV == 0:
                        pe.wait_ge(qT_ready, g // KV + 1)
                        pe.wait_ge(k_ready, g // KV + 1)
                    if g >= DEEP:
                        pe.wait_ge(exp_ready, g - DEEP + 1)
                    k_, q_ = k_own[g // KV % 2], qT[g // KV]
                    product(ps_score[g % DEEP], [(k_[:, g % KV, half], q_) for half in range(2)]
                            ).then_inc(score_ps, 1)
                elif step == "value":
                    group, j = g // KV, g % KV
                    if g == 0:
                        pe.wait_ge(qkn_ready, GROUPS)
                    if g == KV:
                        pe.wait_ge(qT_ready, GROUPS)
                    if j == 0 and group >= 2:
                        pe.wait_ge(oT_ready, group - 1)
                    pe.wait_ge(v_ready, group + 1)
                    pe.wait_ge(prob_ready[g % 2], g // 2 + 1)
                    nc.tensor.matmul(ps_value[group % 2][WIDE * j:WIDE * (j + 1), :], v_one[:, group, j],
                                     probs[g % DEEP].rearrange("p r t -> p (r t)"), start=True,
                                     stop=True).then_inc(value_ps, 1)
                elif step == "out_t":
                    pe.wait_ge(oT_ready, g + 1)
                    if g == 0:
                        pe.wait_ge(kT_ready, GROUPS)
                    else:
                        pe.wait_ge(attn_ready, g)
                    for r in range(REP):
                        last = nc.tensor.transpose(ps_out[:, r * P:(r + 1) * P], oT[:, r * T:(r + 1) * T], id_sb[:])
                    last.then_inc(out_ps, 1)
                elif step == "attn_t":
                    pe.wait_ge(attn_ready, g + 1)
                    if g >= 1:
                        pe.wait_ge(h2_ready, g)
                    flat = attn[:].rearrange("p h d -> p (h d)")
                    for k in range(KH):
                        last = nc.tensor.transpose(ps_attnT[:, k * T:(k + 1) * T], flat[:, k * P:(k + 1) * P],
                                                   id_sb[0:T, 0:T])
                    last.then_inc(attnT_ps, 1)
                elif step == "project":
                    pe.wait_ge(attnT_l, g + 1)
                    product(ps_proj, split(KH, (lambda k: attnT_hi[:, k], lambda k: attnT_lo[:, k]),
                                           (lambda k: proj_w[0][:, k], lambda k: proj_w[1][:, k]))
                            ).then_inc(proj_ps, 1)
                elif step == "seed":
                    pe.wait_ge(oT_ready, GROUPS)
                    pe.wait_ge(attn_ready, GROUPS)
                    pe.wait_ge(h2_ready, GROUPS)
                    for c in range(2):
                        for hid in range(KH):
                            first = True
                            for g in range(GROUPS):
                                lo, hi = max(g * T, c * HALF), min((g + 1) * T, (c + 1) * HALF)
                                if lo < hi:
                                    nc.tensor.matmul(ps_y[c][hid][:, lo - c * HALF:hi - c * HALF],
                                                     h_all[:, g, hid * P:(hid + 1) * P],
                                                     id_sb[0:T, lo - g * T:hi - g * T], start=first, stop=False,
                                                     skip_group_check=True)
                                    first = False
                elif step == "ffn_t":
                    if g == 0:
                        pe.wait_ge(exp_ready, GROUPS * KV)
                    if g >= 2:
                        pe.wait_ge(x2_l, g - 1)
                    pe.wait_ge(xn2_ready, g + 1)
                    for k in range(KH):
                        last = nc.tensor.transpose(ps_x2T[g % 2][:, k * T:(k + 1) * T],
                                                   xn2[g % 2][:, k * P:(k + 1) * P], id_sb[0:T, 0:T])
                    last.then_inc(x2T_ps, 1)
                elif step == "logits":
                    pe.wait_ge(x2_l, g + 1)
                    at = slice(g * T, (g + 1) * T)
                    product(ps_logit[:, g], split(KH, (lambda k: x2_hi[:, k, at], lambda k: x2_lo[:, k, at]),
                                            (lambda k: gate_w[0][:, k], lambda k: gate_w[1][:, k]))
                            ).then_inc(logit_ps, 1)

            def down_product(u):
                e, unit = u // UNITS, u % UNITS
                c, m = unit // MT, unit % MT
                b = e % 2
                pe.wait_ge(mid_l, u + 1)
                for hid in range(KH):
                    for w, h in ((w_hi, mid_hi), (w_hi, mid_lo), (w_lo, mid_hi)):
                        last = nc.tensor.matmul(ps_y[c][hid], down(w[b], m, hid), h[u % HBUF], start=False,
                                                stop=False, skip_group_check=True)
                last.then_inc(downed, 1)

            pe.wait_ge(x2_l, GROUPS)
            for e in range(EXPERTS + 1):
                for unit in range(UNITS):
                    u = e * UNITS + unit
                    c, m = unit // MT, unit % MT
                    b = e % 2
                    chunk = slice(c * HALF, (c + 1) * HALF)
                    if unit == 0:
                        pe.wait_ge(we_lo, (e + 1) * PIECES)
                    if u == 0:
                        pe.wait_ge(logit_ready, 2)
                    if u >= 2:
                        pe.wait_ge(silu_ready, u - 1)
                        pe.wait_ge(mid_ready, u - 1)
                    if u == COEF_UNIT:
                        pe.wait_ge(silu_ready, u)
                        pe.wait_ge(coef_ready, 1)
                        for g in range(GROUPS):
                            at = (g % 3) * T
                            last = nc.tensor.transpose(banks[g // 3][0:EXPERTS, at:at + T], coef[:, g],
                                                       id_sb[0:T, 0:T])
                        last.then_inc(coefT_ps, 1)
                        pe.wait_ge(coefT_ready, 2)
                    for matrix, dst in ((0, ps_gate), (1, ps_up)):
                        last = product(dst[u % 2],
                                       split(KH, (lambda k: gate_up(w_hi[b], matrix, k, m),
                                                  lambda k: gate_up(w_lo[b], matrix, k, m)),
                                             (lambda k: x2_hi[:, k, chunk], lambda k: x2_lo[:, k, chunk])))
                    last.then_inc(gu_ps, 1)
                    if u >= LAG:
                        down_product(u - LAG)
            for u in range((EXPERTS + 1) * UNITS - LAG, (EXPERTS + 1) * UNITS):
                down_product(u)


def kernel(**inputs):
    import concourse.bacc as bacc
    from concourse.bass_utils import run_bass_kernel_spmd as run

    f = np.float32
    side = IMAGE // PATCH
    x = np.ascontiguousarray(inputs["x"])
    patches = x.reshape(BATCH, CHANNELS, side, PATCH, side, PATCH).transpose(0, 1, 3, 5, 2, 4)
    patches = patches.reshape(BATCH, PATCHES, FLAT).transpose(2, 0, 1)
    xt = np.zeros((FLAT, GROUPS * PER_GROUP, SEQ), f)
    xt[:, :BATCH, 1:] = patches
    xt = xt.reshape(KF, P, GROUPS, T).transpose(1, 2, 0, 3)
    clsrows = np.zeros((T, HID), f)
    clsrows[::SEQ] = inputs["cls_tok"][0, 0]

    def rows(w, k):
        return np.asarray(w).reshape(k, P, -1).transpose(1, 0, 2).reshape(P, -1)

    wq = np.asarray(inputs["L0_attn_Wq"]).reshape(KV, REP, D, HID).transpose(1, 0, 2, 3).reshape(HID, HID)
    wqkv = np.concatenate([wq, inputs["L0_attn_Wkv"]], 0).T
    wproj = np.asarray(inputs["L0_attn_Wproj"]).T.reshape(KV, REP, D, HID).transpose(1, 0, 2, 3).reshape(HID, HID)

    def expert(gate, up, dn):
        return np.concatenate([rows(gate, KH), rows(up, KH), rows(dn, MT)], 1)

    experts = np.stack([expert(inputs["L0_ffn_gate_proj_w"][e], inputs["L0_ffn_up_proj_w"][e],
                               inputs["L0_ffn_down_proj_w"][e]) for e in range(EXPERTS)])
    shared = expert(inputs["L0_ffn_shared_gate_w"][0], inputs["L0_ffn_shared_up_w"][0],
                    inputs["L0_ffn_shared_down_w"][0])
    theta = (1.0 / 10000.0 ** (np.arange(0, D, 2, dtype=f) / f(D))).astype(f)
    pos = np.tile(np.arange(SEQ, dtype=f), PER_GROUP)
    freqs = np.outer(pos, theta).astype(f)
    cos = np.concatenate([np.cos(freqs)] * 2, 1).astype(f)
    sin = np.concatenate([-np.sin(freqs), np.sin(freqs)], 1).astype(f)
    t = np.arange(T)
    mask = ((t[:, None] // SEQ == t[None] // SEQ) & (t[:, None] <= t[None])).astype(f)
    e = np.arange(EXPERTS)
    before = np.broadcast_to((e[None, :] < e[:, None]).astype(f), (T, EXPERTS, EXPERTS))

    arrays = {"x_in": xt, "cls_in": clsrows, "w_tok_in": rows(inputs["L0_tok_W"], KF), "w_qkv_in": rows(wqkv, KH),
              "w_proj_in": rows(wproj, KH), "w_gate_in": rows(np.asarray(inputs["L0_ffn_gate_w"]).T, KH),
              "beta_in": np.asarray(inputs["L0_ffn_beta"]), "w_exp_in": experts, "w_sh_in": shared,
              "rope_in": np.concatenate([cos, sin], 1), "mask_in": mask, "ident_in": np.eye(P, dtype=f), "before_in": before}
    arrays = {k: np.ascontiguousarray(v) for k, v in arrays.items()}
    nc = bacc.Bacc("TRN2", target_bir_lowering=False, num_devices=1)
    args = [nc.dram_tensor(k, v.shape, mybir.dt.from_np(v.dtype), kind="ExternalInput").ap()
            for k, v in arrays.items()]
    c_dram = nc.dram_tensor("coef_scratch", (EXPERTS, TOKENS), F32, kind="Internal").ap()
    out = nc.dram_tensor("out_dram", (HID, TOKENS), F32, kind="ExternalOutput").ap()
    vit_block(nc, *args, c_dram, out)
    r = run(nc, [arrays], core_ids=[0])
    got = r.results[0]["out_dram"]
    return np.ascontiguousarray(got.reshape(HID, BATCH, SEQ).transpose(1, 2, 0))
```

```python
from contextlib import ExitStack

import concourse.bass as bass
import numpy as np
from concourse import mybir

F32 = mybir.dt.float32
F32R = mybir.dt.float32r
ALU = mybir.AluOpType
ACT = mybir.ActivationFunctionType
AX_X = mybir.AxisListType.X

P = 128
BATCH, CHANNELS, IMAGE, PATCH = 16, 3, 96, 16
HID = 256
PATCHES = (IMAGE // PATCH) ** 2
SEQ = PATCHES + 1
TOKENS = BATCH * SEQ
FLAT = CHANNELS * PATCH * PATCH
KF = FLAT // P
KH = HID // P
PER_GROUP = P // SEQ
T = PER_GROUP * SEQ
GROUPS = -(-BATCH // PER_GROUP)
PADDED = GROUPS * T
HEADS, KV, D = 16, 4, 16
REP = HEADS // KV
QKV = HID + 2 * KV * D
WIDE = 2 * D
EXPERTS, MID = 8, 512
TOP = 2
MT = MID // P
LN_EPS = 1e-5
QK_EPS = 1e-6
SCALE = 1.0 / D ** 0.5
MASKED = -32768.0
HALF = TOKENS // 2
EXPERT_COLS = 3 * KH * MID
PIECES = 6
PIECE = EXPERT_COLS // PIECES
UNITS = 2 * MT
PAIR_UNITS = 2 * UNITS
LAST_PAIR = EXPERTS // 2
LAG = 2
DEEP = 4
SCORES = 3
XBUF = 4
HBUF = 4


def later(i, v, n):
    return not (isinstance(i, int) and i == 0) or v >= n


PERIOD = 5.91
PROJECTIONS = {
    "x_high": -1.59, "x_low": -1.55, "embed_a": 13.96, "embed_b": 16.50, "ln_add": 18.54, "ln_stats": 19.01,
    "ln_mean": 19.58, "ln_root": 20.62, "ln_inverse": 21.93, "ln_apply": 22.74, "norm_t": 23.69,
    "norm_high": 23.70, "norm_low": 24.88, "qkv": 27.67, "qk_square": 28.90, "v_copy": 31.75, "qk_sum": 29.68,
    "qk_root": 30.49, "qk_eps": 30.93, "qk_inverse": 33.29, "qk_apply": 34.46, "turn": 37.32, "rotate": 38.14,
    "heads_high": 40.24, "heads_low": 40.97, "heads_t": 42.60, "heads_copy": 43.38}
START = 5.97
SLOT = 1.2
PAIR = {
    "score": -2.16, "exp": -0.35, "value": 2.76}
ATTENTION = {
    "spread_k": -5.24, "split_w": 4.00, "o_copy": 5.96, "out_t": 7.12, "attend": 7.41, "attn_t": 10.35,
    "attn_high": 10.82, "attn_low": 10.96, "project": 12.33, "residual": 13.65, "ln2_root": 14.84,
    "ln2_apply": 15.73, "ffn_t": 19.39, "ffn_high": 20.04, "ffn_low": 20.91, "logits": 22.14,
    "read_logits": 22.26, "compare": 22.62, "rank": 23.10}
ONCE = {
    ("tok_high", 0): 2.19, ("tok_low", 0): 5.93, ("tok_high", 1): 2.65, ("tok_low", 1): 13.52,
    ("small_high", 0): 5.67, ("small_low", 0): 20.46, ("mask_copy", 0): 28.99}
UNIT_AT = [37.89, 40.64, 46.19, 67.02, 71.48, 108.20, 121.87, 135.67]
UNIT = {
    "gate_up": 7.98, "down": 16.32, "silu": 15.80, "mid": 17.10, "next_high": 17.92, "next_low": 25.79,
    "mid_high": 17.22, "mid_low": 25.68}
SHARED = {
    ("seed", 0): 40.30, ("route", 0): 55.33, ("coef_t", 0): 77.31, ("coef_copy", 0): 81.18, ("seed", 1): 110.00,
    ("mid", 0): 35.47, ("mid_high", 0): 41.93, ("mid_low", 0): 42.96, ("gate_up", 0): 30.77, ("silu", 0): 32.94,
    ("gate_up", 1): 36.92, ("silu", 1): 37.66, ("mid", 1): 38.51, ("mid_high", 1): 44.41, ("mid_low", 1): 50.02,
    ("gate_up", 2): 49.48, ("down", 2): 49.63, ("silu", 2): 49.55, ("mid", 2): 54.70, ("mid_high", 2): 56.99,
    ("mid_low", 2): 60.62, ("gate_up", 3): 75.00, ("down", 3): 82.68, ("silu", 3): 78.90, ("mid", 3): 79.62,
    ("mid_high", 3): 79.67, ("mid_low", 3): 80.84}


def schedule():
    at = dict(ONCE)
    for g in range(GROUPS):
        at.update({(step, g): PERIOD * g + t for step, t in PROJECTIONS.items()})
    start = at["qk_root", GROUPS - 1] + START
    for g in range(GROUPS):
        at.update({(step, g): start + SLOT * (KV * g + t) for step, t in ATTENTION.items()})
    for n in range(GROUPS * KV):
        at.update({(step, n): start + SLOT * (n + t) for step, t in PAIR.items()})
    for u in range(UNITS):
        at.update({(step, u): start + SLOT * (UNIT_AT[u] + t) for step, t in UNIT.items()})
    at.update({step: start + SLOT * t for step, t in SHARED.items()})
    return sorted(at, key=at.get)


def vit_block(nc, x, clsrows, w_tok, w_qkv, w_proj, w_gate, beta, w_exp, w_sh, rope, mask, ident,
              before, c_dram, out):
    with ExitStack() as ctx:
        def sb(name, shape, dt=F32):
            return ctx.enter_context(nc.sbuf_tensor(name, shape, dt))

        def sem(name):
            return ctx.enter_context(nc.semaphore(name))

        banks = [ctx.enter_context(nc.psum_tensor(f"bank{i}", [P, 512], F32)) for i in range(8)]

        early_late = sb("early_late", [P, max(GROUPS * KF * T, EXPERTS * TOKENS)])
        xraw = early_late[:, 0:GROUPS * KF * T].rearrange("p (g k t) -> p g k t", g=GROUPS, k=KF)
        split_hi = [sb(f"split_hi{i}", [P, KF * T], F32R) for i in range(2)]
        split_lo = [sb(f"split_lo{i}", [P, KF * T], F32R) for i in range(2)]
        small_raw = sb("small_raw", [P, KF * HID + KH * (QKV + HID + EXPERTS)])
        small_hi = sb("small_hi", [P, KF * HID + KH * (QKV + HID + EXPERTS)], F32R)
        small_lo = sb("small_lo", [P, KF * HID + KH * (QKV + HID + EXPERTS)], F32R)
        cls_sb = sb("cls_sb", [T, HID])
        beta_sb = sb("beta_sb", [T, EXPERTS])
        rope_sb = sb("rope_sb", [T, 2 * D])
        cos_sb, sin_sb = rope_sb[:, 0:D], rope_sb[:, D:2 * D]
        mask_sb = sb("mask_sb", [T, T])
        mask_r = sb("mask_r", [T, REP, T], F32R)
        id_r = sb("id_r", [T, T], F32R)
        id_sb = sb("id_sb", [P, P])
        before_sb = sb("before_sb", [T, EXPERTS, EXPERTS])

        def weights(t, at, k, n):
            return t[:, at:at + k * n].rearrange("p (k n) -> p k n", k=k)

        at_qkv = KF * HID
        at_proj = at_qkv + KH * QKV
        at_gate = at_proj + KH * HID
        tok_w = [weights(t, 0, KF, HID) for t in (small_hi, small_lo)]
        qkv_w = [weights(t, at_qkv, KH, QKV) for t in (small_hi, small_lo)]
        proj_w = [weights(t, at_proj, KH, HID) for t in (small_hi, small_lo)]
        gate_w = [weights(t, at_gate, KH, EXPERTS) for t in (small_hi, small_lo)]

        h_all = sb("h_all", [T, GROUPS, HID])
        stats = sb("stats", [T, 2, GROUPS, 6])
        moments = sb("moments", [T, 2, GROUPS, 2])
        deviation = sb("deviation", [T, 2, GROUPS])
        rstd = sb("rstd", [T, 2, GROUPS])
        ln_eps = sb("ln_eps", [T, 1])
        early_root = sb("early_root", [T, 1])
        minus_half = sb("minus_half", [T, 1])
        xn = sb("xn", [T, HID])
        xnT_hi = sb("xnT_hi", [P, KH, T], F32R)
        xnT_lo = sb("xnT_lo", [P, KH, T], F32R)
        squares = sb("squares", [T, HEADS + KV, D])
        norm2 = sb("norm2", [T, HEADS + KV])
        root = sb("root", [T, HEADS + KV])
        norm = sb("norm", [T, HEADS + KV])
        inv_norm = sb("inv_norm", [T, HEADS + KV])
        qkn = sb("qkn", [T, HEADS + KV, D])
        turned = [sb(f"turned{i}", [T, HEADS + KV, D]) for i in range(2)]
        rot = [sb(f"rot{i}", [T, HEADS + KV, D]) for i in range(2)]
        heads = sb("heads", [T, HEADS + 2 * KV, WIDE])
        v_one = sb("v_one", [T, GROUPS, KV, WIDE])
        kT = [sb(f"kT{g}", [P, 2, T], F32R) for g in range(GROUPS)]
        k_own = [sb(f"k_own{i}", [P, KV, 2, T], F32R) for i in range(2)]
        attn_ffn = [sb(f"attn_ffn{i}", [P, REP * T]) for i in range(DEEP)]
        probs = [t[0:T].rearrange("p (r t) -> p r t", r=REP) for t in attn_ffn]
        oT = sb("oT", [P, REP * T])
        inv_den = sb("inv_den", [T, HEADS])
        attn = sb("attn", [T, HEADS, D])
        attnT_hi = sb("attnT_hi", [P, KH, T], F32R)
        attnT_lo = sb("attnT_lo", [P, KH, T], F32R)
        xn2 = [sb(f"xn2{i}", [T, HID]) for i in range(2)]
        x2_hi = sb("x2_hi", [P, KH, PADDED], F32R)
        x2_lo = sb("x2_lo", [P, KH, PADDED], F32R)
        logits = sb("logits", [T, GROUPS, EXPERTS])
        biased = sb("biased", [T, GROUPS, EXPERTS])

        greater = sb("greater", [T, EXPERTS, EXPERTS])
        equal = sb("equal", [T, EXPERTS, EXPERTS])
        chosen = sb("chosen", [T, GROUPS, EXPERTS])
        rank = sb("rank", [T, GROUPS, EXPERTS])
        half_tanh = sb("half_tanh", [T, GROUPS, EXPERTS])
        sigm = sb("sigm", [T, GROUPS, EXPERTS])
        coef = sb("coef", [T, GROUPS, EXPERTS])
        coefT = sb("coefT", [EXPERTS, PADDED])
        cbc = early_late[:, 0:EXPERTS * TOKENS].rearrange("p (e t) -> p e t", e=EXPERTS)

        wraw = [sb(f"wraw{i}", [P, EXPERT_COLS]) for i in range(2)]
        w_hi = [sb(f"w_hi{i}", [P, EXPERT_COLS], F32R) for i in range(2)]
        w_lo = [sb(f"w_lo{i}", [P, EXPERT_COLS], F32R) for i in range(2)]
        more = [w_hi[1][:, i * KF * T:(i + 1) * KF * T] for i in range(4)]
        x_hi = [t.rearrange("p (k t) -> p k t", k=KF) for t in (split_hi[0][:], split_hi[1][:], more[0], more[1])]
        x_lo = [t.rearrange("p (k t) -> p k t", k=KF) for t in (split_lo[0][:], split_lo[1][:], more[2], more[3])]
        qT = [w_lo[1][:, g * REP * T:(g + 1) * REP * T] for g in range(GROUPS)]
        silu = [attn_ffn[i][:, 0:HALF] for i in range(2)]
        upc = [attn_ffn[2 + i][:, 0:HALF] for i in range(2)]
        mid = [sb(f"mid{i}", [P, HALF]) for i in range(2)]
        mid_hi, mid_lo = ([t[:, i * HALF:(i + 1) * HALF] for t in two for i in range(2)]
                          for two in (split_hi, split_lo))
        result = small_raw[:, 0:KH * TOKENS].rearrange("p (c k t) -> p c k t", c=2, k=KH)

        def gate_up(t, matrix, k, m):
            at = (matrix * KH + k) * MID + m * P
            return t[:, at:at + P]

        def down(t, m, hid):
            at = 2 * KH * MID + m * HID + hid * P
            return t[:, at:at + P]

        ps_embed = [banks[0][0:T, 0:HID], banks[1][0:T, 0:HID]]
        ps_xnT = banks[2][:, 0:KH * T]
        ps_qkv = [banks[3][0:T, 0:QKV], banks[4][0:T, 0:QKV]]
        ps_qT = banks[5][:, 0:REP * T]
        ps_kT = banks[6][:, 0:2 * T]
        ps_score = [banks[i][0:T, 0:REP * T] for i in range(SCORES)]
        ps_value = [banks[4][:, 0:REP * T], banks[5][:, 0:REP * T]]
        ps_out = banks[6][0:T, :]
        ps_attnT = banks[7][:, 0:KH * T]
        ps_proj = banks[7][0:T, 256:256 + HID]
        router_bank = [banks[3]] * (GROUPS - 2) + [banks[4], banks[6]]
        ps_x2T = [bank[:, 0:KH * T] for bank in router_bank]
        ps_logit = [bank[0:T, KH * T:KH * T + EXPERTS] for bank in router_bank]
        ps_coefT = [bank[0:EXPERTS, 0:3 * T] for bank in (banks[6], banks[7])]
        ps_gate = [banks[0][:, 0:HALF], banks[1][:, 0:HALF]]
        ps_up = [banks[2][:, 0:HALF], banks[3][:, 0:HALF]]
        ps_y = [[banks[4 + 2 * c + hid][:, 0:HALF] for hid in range(KH)] for c in range(2)]

        d_x = [sem(f"d_x{g}") for g in range(GROUPS)]
        d_tok = [sem("d_tok0"), sem("d_tok1")]
        d_small = sem("d_small")
        d_cls = sem("d_cls")
        d_id = sem("d_id")
        d_rope = sem("d_rope")
        d_mask = sem("d_mask")
        d_late = sem("d_late")
        d_shared = sem("d_shared")
        d_expert = [sem("d_expert0"), sem("d_expert1")]
        d_coef = sem("d_coef")
        d_cbc = sem("d_cbc")
        d_cbc_rest = sem("d_cbc_rest")
        d_out = sem("d_out")

        ws_hi = sem("ws_hi")
        ws_lo = sem("ws_lo")
        fill = sem("fill")
        xs_hi = sem("xs_hi")
        xs_lo = sem("xs_lo")
        embedded = sem("embedded")
        h_ready = sem("h_ready")
        xn_ready = sem("xn_ready")
        ln1_stats = sem("ln1_stats")
        ln2_stats = sem("ln2_stats")
        ln1_root = sem("ln1_root")
        ln2_root = sem("ln2_root")
        variance_eps = sem("variance_eps")
        norm2_ready = sem("norm2_ready")
        root_ready = sem("root_ready")
        xnT_ps = sem("xnT_ps")
        xnT_h = sem("xnT_h")
        xnT_l = sem("xnT_l")
        qkv_ps = sem("qkv_ps")
        sq_ready = sem("sq_ready")
        v_ready = sem("v_ready")
        qkn_ready = sem("qkn_ready")
        turned_ready = sem("turned_ready")
        rot_ready = sem("rot_ready")
        heads_h = sem("heads_h")
        heads_l = sem("heads_l")
        heads_ps = sem("heads_ps")
        zeroed = sem("zeroed")
        k_ready = sem("k_ready")
        qT_ready = sem("qT_ready")
        kT_ready = sem("kT_ready")
        score_ps = sem("score_ps")
        exp_ready = sem("exp_ready")
        mask_ready = sem("mask_ready")
        value_ps = sem("value_ps")
        oT_ready = sem("oT_ready")
        out_ps = sem("out_ps")
        attn_ready = sem("attn_ready")
        attnT_ps = sem("attnT_ps")
        attnT_h = sem("attnT_h")
        attnT_l = sem("attnT_l")
        proj_ps = sem("proj_ps")
        h2_ready = sem("h2_ready")
        xn2_ready = sem("xn2_ready")
        x2T_ps = sem("x2T_ps")
        x2_h = sem("x2_h")
        x2_l = sem("x2_l")
        logit_ps = sem("logit_ps")
        logit_ready = sem("logit_ready")
        tanh_ready = sem("tanh_ready")
        compared = sem("compared")
        ranked = sem("ranked")
        coef_ready = sem("coef_ready")
        coefT_ps = sem("coefT_ps")
        coefT_ready = sem("coefT_ready")
        pool_step = sem("pool_step")
        dve_step = sem("dve_step")
        we_hi = sem("we_hi")
        we_lo = sem("we_lo")
        gu_ps = sem("gu_ps")
        silu_ready = sem("silu_ready")
        up_read = sem("up_read")
        mid_ready = sem("mid_ready")
        mid_h = sem("mid_h")
        mid_l = sem("mid_l")
        downed = sem("downed")
        y_ready = sem("y_ready")

        block = ctx.enter_context(nc.Block())
        ORDER = schedule()

        @block.sync
        def _(sp):
            n_tok = KF * HID
            sp.dma_start(xraw[:, 0], x[:, 0]).then_inc(d_x[0], 16)
            for half in range(2):
                at = slice(half * n_tok // 2, (half + 1) * n_tok // 2)
                sp.dma_start(small_raw[:, at], w_tok[:, at]).then_inc(d_tok[half], 16)
            sp.dma_start(cls_sb[:], clsrows).then_inc(d_cls, 16)
            sp.dma_start(id_sb[:], ident).then_inc(d_id, 16)
            sp.dma_start(small_raw[:, at_qkv:at_proj], w_qkv).then_inc(d_small, 16)
            for g in range(1, GROUPS):
                sp.dma_start(xraw[:, g], x[:, g]).then_inc(d_x[g], 16)
                if g == 1:
                    sp.dma_start(rope_sb[:], rope).then_inc(d_rope, 16)
                    sp.dma_start(mask_sb[:], mask).then_inc(d_mask, 16)
                    sp.dma_start(small_raw[:, at_proj:at_gate], w_proj).then_inc(d_small, 16)
                    sp.dma_start(small_raw[:, at_gate:], w_gate).then_inc(d_small, 16)
            sp.dma_start(wraw[0][:], w_sh).then_inc(d_shared, 16)
            sp.dma_start(wraw[1][:], w_exp[0]).then_inc(d_expert[0], 16)
            sp.wait_ge(we_lo, PIECES)
            sp.dma_start(wraw[0][:], w_exp[1]).then_inc(d_expert[1], 16)
            sp.wait_ge(coefT_ready, 2)
            sp.dma_start(c_dram, coefT[:, 0:TOKENS]).then_inc(d_coef, 16)
            sp.wait_ge(d_coef, 16)
            sp.dma_start(cbc[:, 0:1], c_dram[0:1].partition_broadcast(P)).then_inc(d_cbc, 16)
            sp.dma_start(cbc[:, 1:], c_dram[1:].partition_broadcast(P)).then_inc(d_cbc_rest, 16)
            with sp.Fori(0, LAST_PAIR - 1) as j:
                for parity in range(2):
                    sp.wait_ge(we_lo, j * (2 * PIECES) + (parity + 2) * PIECES)
                    sp.dma_start(wraw[1 - parity][:], w_exp[2 * j + (parity + 2)]).then_inc(d_expert[parity], 16)
            for c in range(2):
                sp.wait_ge(y_ready, KH * (c + 1))
                sp.dma_start(out[:, :, c * HALF:(c + 1) * HALF], result[:, c]).then_inc(d_out, 16)
            sp.wait_ge(d_out, 32)

        @block.gpsimd
        def _(pool):
            steps = [0]

            def settle(ins):
                steps[0] += 1
                ins.then_inc(pool_step, 1)
                pool.wait_ge(pool_step, steps[0])

            for i in range(2):
                pool.memset(k_own[i][:].bitcast(mybir.dt.uint32), 0).then_inc(zeroed, 1)
            pool.memset(minus_half[:], -0.5).then_inc(zeroed, 1)
            pool.wait_ge(zeroed, 3)
            pool.dma_start(before_sb[:], before).then_inc(d_late, 16)
            pool.dma_start(beta_sb[:], beta.partition_broadcast(T)).then_inc(d_late, 16)
            for step, g in ORDER:
                if step == "x_low":
                    pool.wait_ge(xs_hi, g + 1)
                    if g >= XBUF:
                        pool.wait_ge(embedded, g - XBUF + 1)
                    nc.gpsimd.tensor_tensor(x_lo[g % XBUF], xraw[:, g], x_hi[g % XBUF].bitcast(F32),
                                            ALU.subtract).then_inc(xs_lo, 1)
                elif step == "turn":
                    if g == 0:
                        pool.wait_ge(d_rope, 16)
                    pool.wait_ge(qkn_ready, g + 1)
                    if g >= 2:
                        pool.wait_ge(heads_l, g - 1)
                    nc.gpsimd.tensor_tensor(rot[g % 2][:], qkn[:], cos_sb[:, None, :].broadcast_to([T, HEADS + KV, D]),
                                            ALU.mult)
                    nc.gpsimd.tensor_tensor(
                        turned[g % 2][:, :, 0:D // 2], qkn[:, :, D // 2:D],
                        sin_sb[:, None, 0:D // 2].broadcast_to([T, HEADS + KV, D // 2]), ALU.mult)
                    nc.gpsimd.tensor_tensor(
                        turned[g % 2][:, :, D // 2:D], qkn[:, :, 0:D // 2],
                        sin_sb[:, None, D // 2:D].broadcast_to([T, HEADS + KV, D // 2]),
                        ALU.mult).then_inc(turned_ready, 1)
                elif step == "ln2_root":
                    pool.wait_ge(ln2_stats, g + 1)
                    nc.gpsimd.tensor_scalar(deviation[:, 1, g:g + 1], moments[:, 1, g, 1:2], LN_EPS, None,
                                            ALU.add).then_inc(variance_eps, 1)
                    pool.wait_ge(variance_eps, g + 1)
                    nc.gpsimd.tensor_tensor(rstd[:, 1, g:g + 1], deviation[:, 1, g:g + 1], minus_half[:],
                                            ALU.pow).then_inc(ln2_root, 1)
                elif step == "rank":
                    if g == 0:
                        pool.wait_ge(d_late, 32)
                    pool.wait_ge(compared, g + 1)
                    settle(nc.gpsimd.tensor_tensor(equal[:], equal[:], before_sb[:], ALU.mult))
                    settle(nc.gpsimd.tensor_tensor(greater[:], greater[:], equal[:], ALU.add))
                    settle(nc.gpsimd.tensor_tensor(greater[:, :, 0:4], greater[:, :, 0:4], greater[:, :, 4:8], ALU.add))
                    settle(nc.gpsimd.tensor_tensor(greater[:, :, 0:2], greater[:, :, 0:2], greater[:, :, 2:4], ALU.add))
                    nc.gpsimd.tensor_tensor(rank[:, g], greater[:, :, 0], greater[:, :, 1], ALU.add).then_inc(ranked, 1)
                elif step == "route":
                    pool.wait_ge(ranked, GROUPS)
                    settle(nc.gpsimd.tensor_scalar(chosen[:], rank[:], TOP - 0.5, None, ALU.is_lt))
                    pool.wait_ge(tanh_ready, 1)
                    settle(nc.gpsimd.tensor_scalar(sigm[:], half_tanh[:], 0.5, 0.5, ALU.mult, ALU.add))
                    nc.gpsimd.tensor_tensor(coef[:], chosen[:], sigm[:], ALU.mult).then_inc(coef_ready, 1)

        @block.scalar
        def _(act):
            def copy(dst, src):
                return nc.scalar.activation(dst, src, ACT.Copy)


            act.wait_ge(fill, 2)
            nc.scalar.activation(early_root[:], ln_eps[:], ACT.Sqrt)

            def weights_hi(b, piece):
                at = slice(piece * PIECE, (piece + 1) * PIECE)
                copy(w_hi[b][:, at], wraw[b][:, at]).then_inc(we_hi, 1)

            def silu_of_gate(i, v):
                u = i * PAIR_UNITS + v
                act.wait_ge(gu_ps, u + 1)
                if isinstance(u, int) and u == 0:
                    act.wait_ge(value_ps, GROUPS * KV)
                if later(i, v, 2):
                    act.wait_ge(mid_ready, u - 1)
                nc.scalar.activation(silu[v % 2], ps_gate[v % 2], ACT.Silu).then_inc(silu_ready, 1)

            def next_high(i, v):
                unit = v % UNITS
                if 1 <= unit <= PIECES:
                    if unit == 1:
                        act.wait_ge(d_expert[v // UNITS], i * 16 + 16)
                        if later(i, v, UNITS):
                            act.wait_ge(downed, i * PAIR_UNITS + v - 1)
                    weights_hi((v // UNITS + 1) % 2, unit - 1)

            def mid_high(i, v):
                u = i * PAIR_UNITS + v
                act.wait_ge(mid_ready, u + 1)
                if later(i, v, HBUF):
                    act.wait_ge(downed, u - HBUF + 1)
                copy(mid_hi[v % HBUF], mid[v % 2][:]).then_inc(mid_h, 1)

            def expert_unit(i, v):
                silu_of_gate(i, v)
                if not (isinstance(i, int) and i == LAST_PAIR):
                    next_high(i, v)
                mid_high(i, v)

            for step, g in ORDER:
                if step == "tok_high":
                    act.wait_ge(d_tok[g], 16)
                    at = slice(g * at_qkv // 2, (g + 1) * at_qkv // 2)
                    copy(small_hi[:, at], small_raw[:, at]).then_inc(ws_hi, 1)
                elif step == "x_high":
                    act.wait_ge(d_x[g], 16)
                    if g >= XBUF:
                        act.wait_ge(embedded, g - XBUF + 1)
                    copy(x_hi[g % XBUF], xraw[:, g]).then_inc(xs_hi, 1)
                elif step == "small_high":
                    act.wait_ge(d_small, 48)
                    copy(small_hi[:, at_qkv:], small_raw[:, at_qkv:]).then_inc(ws_hi, 1)
                elif step == "mask_copy":
                    act.wait_ge(d_mask, 16)
                    act.wait_ge(d_id, 16)
                    copy(mask_r[:], mask_sb[:, None, :].broadcast_to([T, REP, T]))
                    copy(id_r[:], id_sb[0:T, 0:T]).then_inc(mask_ready, 1)
                elif step == "norm_high":
                    act.wait_ge(xnT_ps, g + 1)
                    if g >= 1:
                        act.wait_ge(qkv_ps, g)
                    copy(xnT_hi[:].rearrange("p k t -> p (k t)"), ps_xnT).then_inc(xnT_h, 1)
                elif step == "ln_root":
                    if g == 0:
                        act.wait_ge(fill, 2)
                    act.wait_ge(ln1_stats, g + 1)
                    nc.scalar.activation(deviation[:, 0, g:g + 1], moments[:, 0, g, 1:2], ACT.Sqrt,
                                         bias=ln_eps[:, 0:1]).then_inc(ln1_root, 1)
                elif step == "qk_square":
                    act.wait_ge(qkv_ps, g + 1)
                    if g >= 1:
                        act.wait_ge(norm2_ready, g)
                    nc.scalar.activation(squares[:].rearrange("p h d -> p (h d)"),
                                         ps_qkv[g % 2][:, 0:HID + KV * D], ACT.Square).then_inc(sq_ready, 1)
                elif step == "v_copy":
                    copy(v_one[:, g, :, 0:D], ps_qkv[g % 2][:, HID + KV * D:QKV].rearrange(
                        "p (j d) -> p j d", j=KV)).then_inc(v_ready, 1)
                elif step == "qk_root":
                    act.wait_ge(norm2_ready, g + 1)
                    nc.scalar.activation(root[:], norm2[:], ACT.Sqrt).then_inc(root_ready, 1)
                elif step == "heads_high":
                    act.wait_ge(rot_ready, g + 1)
                    if g >= 1:
                        act.wait_ge(heads_ps, g)
                    hr = heads[:].bitcast(F32R)
                    copy(hr[:, 0:HEADS, 0:D], rot[g % 2][:, 0:HEADS])
                    k4 = hr[:, HEADS:HEADS + KV].rearrange("p j (two d) -> p j two d", two=2)
                    copy(k4, rot[g % 2][:, HEADS:HEADS + KV, None, :].broadcast_to([T, KV, 2, D])).then_inc(heads_h, 1)
                elif step == "heads_copy":
                    act.wait_ge(heads_ps, g + 1)
                    copy(qT[g], ps_qT).then_inc(qT_ready, 1)
                    copy(kT[g][:].rearrange("p k t -> p (k t)"), ps_kT).then_inc(kT_ready, 1)
                elif step == "exp":
                    act.wait_ge(score_ps, g + 1)
                    if g >= DEEP:
                        act.wait_ge(value_ps, g - DEEP + 1)
                    nc.scalar.activation(probs[g % DEEP].rearrange("p r t -> p (r t)"), ps_score[g % SCORES],
                                         ACT.Exp, scale=SCALE).then_inc(exp_ready, 1)
                elif step == "o_copy":
                    act.wait_ge(value_ps, KV * (g + 1))
                    if g >= 1:
                        act.wait_ge(out_ps, g)
                    copy(oT[:], ps_value[g % 2]).then_inc(oT_ready, 1)
                elif step == "attn_high":
                    act.wait_ge(attnT_ps, g + 1)
                    if g >= 1:
                        act.wait_ge(proj_ps, g)
                    copy(attnT_hi[:].rearrange("p k t -> p (k t)"), ps_attnT).then_inc(attnT_h, 1)
                elif step == "split_w":
                    act.wait_ge(d_shared, 16)
                    weights_hi(0, g)
                elif step == "ffn_high":
                    act.wait_ge(x2T_ps, g + 1)
                    copy(x2_hi[:, :, g * T:(g + 1) * T],
                         ps_x2T[g].rearrange("p (k t) -> p k t", k=KH)).then_inc(x2_h, 1)
                elif step == "route":
                    act.wait_ge(logit_ready, 2 * GROUPS)
                    nc.scalar.activation(half_tanh[:], logits[:], ACT.Tanh, scale=0.5).then_inc(tanh_ready, 1)
                elif step == "coef_copy":
                    act.wait_ge(coefT_ps, 1)
                    copy(coefT[:, 0:3 * T], ps_coefT[0]).then_inc(coefT_ready, 1)
                elif step == "silu":
                    silu_of_gate(0, g)
                elif step == "next_high":
                    next_high(0, g)
                elif step == "mid_high":
                    mid_high(0, g)
            for v in range(UNITS, PAIR_UNITS):
                expert_unit(0, v)
            with act.Fori(1, LAST_PAIR) as i:
                for v in range(PAIR_UNITS):
                    expert_unit(i, v)
            for v in range(UNITS):
                expert_unit(LAST_PAIR, v)
                if v == MT + LAG:
                    act.wait_ge(downed, EXPERTS * UNITS + MT)
                    for hid in range(KH):
                        copy(result[:, 0, hid], ps_y[0][hid]).then_inc(y_ready, 1)
            act.wait_ge(downed, (EXPERTS + 1) * UNITS)
            copy(result[:, 1, 0], ps_y[1][0]).then_inc(y_ready, 1)

        @block.vector
        def _(dve):
            steps = [0]
            mark = {}

            def note(ins, what, g):
                steps[0] += 1
                ins.then_inc(dve_step, 1)
                mark[what, g] = steps[0]

            def after(what, g):
                dve.wait_ge(dve_step, mark[what, g])

            def settle(ins):
                steps[0] += 1
                ins.then_inc(dve_step, 1)
                dve.wait_ge(dve_step, steps[0])

            def statistics(g, which, ready):
                settle(nc.vector.bn_stats(stats[:, which, g], h_all[:, g]))
                nc.vector.bn_aggr(moments[:, which, g], stats[:, which, g]).then_inc(ready, 1)

            def normalize(g, which, dst, ready):
                nc.vector.tensor_scalar(dst, h_all[:, g], moments[:, which, g, 0:1], rstd[:, which, g:g + 1],
                                        ALU.subtract, ALU.mult).then_inc(ready, 1)

            def weights_lo(b, piece, count):
                at = slice(piece * PIECE, (piece + 1) * PIECE)
                dve.wait_ge(we_hi, count)
                nc.vector.tensor_tensor(w_lo[b][:, at], wraw[b][:, at], w_hi[b][:, at].bitcast(F32),
                                        ALU.subtract).then_inc(we_lo, 1)

            def mid_product(i, v):
                u = i * PAIR_UNITS + v
                c = v % UNITS // MT
                dve.wait_ge(gu_ps, u + 1)
                if not later(i, v, UNITS):
                    dve.wait_ge(silu_ready, u + 1)
                    if v >= 2:
                        dve.wait_ge(mid_l, u - 1)
                    nc.vector.tensor_tensor(mid[v % 2][:], ps_up[v % 2], silu[v % 2], ALU.mult).then_inc(mid_ready, 1)
                    return
                if isinstance(u, int) and u == UNITS:
                    dve.wait_ge(d_cbc, 16)
                elif v == 0:
                    dve.wait_ge(d_cbc_rest, 16)
                e = 2 * i + (v // UNITS - 1)
                nc.vector.tensor_tensor(upc[v % 2], ps_up[v % 2], cbc[:, e, c * HALF:(c + 1) * HALF],
                                        ALU.mult).then_inc(up_read, 1)
                dve.wait_ge(silu_ready, u + 1)
                dve.wait_ge(up_read, u - UNITS + 1)
                dve.wait_ge(mid_l, u - 1)
                nc.vector.tensor_tensor(mid[v % 2][:], upc[v % 2], silu[v % 2], ALU.mult).then_inc(mid_ready, 1)

            def next_low(i, v):
                if 1 <= v % UNITS <= PIECES:
                    weights_lo((v // UNITS + 1) % 2, v % UNITS - 1,
                               i * (2 * PIECES) + (v // UNITS + 1) * PIECES + v % UNITS)

            def mid_low(i, v):
                dve.wait_ge(mid_h, i * PAIR_UNITS + v + 1)
                nc.vector.tensor_tensor(mid_lo[v % HBUF], mid[v % 2][:], mid_hi[v % HBUF].bitcast(F32),
                                        ALU.subtract).then_inc(mid_l, 1)

            def expert_unit(i, v):
                mid_product(i, v)
                if not (isinstance(i, int) and i == LAST_PAIR):
                    next_low(i, v)
                mid_low(i, v)

            settle(nc.vector.memset(v_one[:, :, :, D:WIDE], 0.0))
            nc.vector.memset(v_one[:, :, :, D:D + 1], 1.0).then_inc(fill, 1)
            nc.vector.memset(ln_eps[:], LN_EPS).then_inc(fill, 1)
            for step, g in ORDER:
                if step == "tok_low":
                    dve.wait_ge(ws_hi, g + 1)
                    at = slice(g * at_qkv // 2, (g + 1) * at_qkv // 2)
                    nc.vector.tensor_tensor(small_lo[:, at], small_raw[:, at], small_hi[:, at].bitcast(F32),
                                            ALU.subtract).then_inc(ws_lo, 1)
                elif step == "small_low":
                    dve.wait_ge(ws_hi, 3)
                    nc.vector.tensor_tensor(small_lo[:, at_qkv:], small_raw[:, at_qkv:],
                                            small_hi[:, at_qkv:].bitcast(F32), ALU.subtract).then_inc(ws_lo, 1)
                elif step == "ln_add":
                    if g == 0:
                        dve.wait_ge(d_cls, 16)
                    dve.wait_ge(embedded, g + 1)
                    nc.vector.tensor_tensor(h_all[:, g], ps_embed[g % 2], cls_sb[:], ALU.add).then_inc(h_ready, 1)
                elif step == "ln_stats":
                    dve.wait_ge(h_ready, g + 1)
                    note(nc.vector.bn_stats(stats[:, 0, g], h_all[:, g]), step, g)
                elif step == "ln_mean":
                    after("ln_stats", g)
                    nc.vector.bn_aggr(moments[:, 0, g], stats[:, 0, g]).then_inc(ln1_stats, 1)
                elif step == "ln_inverse":
                    dve.wait_ge(ln1_root, g + 1)
                    note(nc.vector.reciprocal(rstd[:, 0, g:g + 1], deviation[:, 0, g:g + 1]), step, g)
                elif step == "ln_apply":
                    if g >= 1:
                        dve.wait_ge(xnT_ps, g)
                    after("ln_inverse", g)
                    normalize(g, 0, xn[:], xn_ready)
                elif step == "norm_low":
                    dve.wait_ge(xnT_h, g + 1)
                    nc.vector.tensor_tensor(xnT_lo[:].rearrange("p k t -> p (k t)"), ps_xnT,
                                            xnT_hi[:].rearrange("p k t -> p (k t)").bitcast(F32),
                                            ALU.subtract).then_inc(xnT_l, 1)
                elif step == "qk_sum":
                    dve.wait_ge(sq_ready, g + 1)
                    nc.vector.reduce_sum(norm2[:], squares[:], AX_X).then_inc(norm2_ready, 1)
                elif step == "qk_eps":
                    dve.wait_ge(root_ready, g + 1)
                    note(nc.vector.tensor_scalar(norm[:], root[:], QK_EPS, None, ALU.add), step, g)
                elif step == "qk_inverse":
                    after("qk_eps", g)
                    note(nc.vector.reciprocal(inv_norm[:], norm[:]), step, g)
                elif step == "qk_apply":
                    after("qk_inverse", g)
                    if g >= 1:
                        dve.wait_ge(turned_ready, g)
                    dve.wait_ge(v_ready, g + 1)
                    nc.vector.tensor_tensor(
                        qkn[:], ps_qkv[g % 2][:, 0:HID + KV * D].rearrange("p (h d) -> p h d", d=D),
                        inv_norm[:, :, None].broadcast_to([T, HEADS + KV, D]), ALU.mult).then_inc(qkn_ready, 1)
                elif step == "rotate":
                    dve.wait_ge(turned_ready, g + 1)
                    nc.vector.tensor_tensor(rot[g % 2][:], rot[g % 2][:], turned[g % 2][:], ALU.add).then_inc(rot_ready, 1)
                elif step == "heads_low":
                    dve.wait_ge(heads_h, g + 1)
                    nc.vector.tensor_tensor(heads[:, 0:HEADS, D:WIDE], rot[g % 2][:, 0:HEADS], heads[:, 0:HEADS, 0:D],
                                            ALU.subtract)
                    k4 = heads[:, HEADS + KV:].rearrange("p j (two d) -> p j two d", two=2)
                    h4 = heads[:, HEADS:HEADS + KV].rearrange("p j (two d) -> p j two d", two=2)
                    nc.vector.tensor_tensor(k4, rot[g % 2][:, HEADS:HEADS + KV, None, :].broadcast_to([T, KV, 2, D]),
                                            h4, ALU.subtract).then_inc(heads_l, 1)
                elif step == "spread_k":
                    dve.wait_ge(kT_ready, g + 1)
                    if g == 0:
                        dve.wait_ge(zeroed, 2)
                    if g >= 2:
                        dve.wait_ge(score_ps, KV * (g - 1))
                    for j in range(KV):
                        rows = slice(WIDE * j, WIDE * (j + 1))
                        last = nc.vector.tensor_copy(k_own[g % 2][rows, j], kT[g][rows])
                    last.then_inc(k_ready, 1)
                elif step == "attend":
                    dve.wait_ge(out_ps, g + 1)
                    o4 = ps_out.rearrange("p (h w) -> p h w", w=WIDE)
                    settle(nc.vector.reciprocal(inv_den[:, :, None], o4[:, :, D:D + 1]))
                    if g >= 1:
                        dve.wait_ge(attnT_ps, g)
                    nc.vector.tensor_tensor(attn[:], o4[:, :, 0:D],
                                            inv_den[:, :, None].broadcast_to([T, HEADS, D]),
                                            ALU.mult).then_inc(attn_ready, 1)
                elif step == "attn_low":
                    dve.wait_ge(attnT_h, g + 1)
                    nc.vector.tensor_tensor(attnT_lo[:].rearrange("p k t -> p (k t)"), ps_attnT,
                                            attnT_hi[:].rearrange("p k t -> p (k t)").bitcast(F32),
                                            ALU.subtract).then_inc(attnT_l, 1)
                elif step == "residual":
                    dve.wait_ge(proj_ps, g + 1)
                    nc.vector.tensor_tensor(h_all[:, g], h_all[:, g], ps_proj, ALU.add).then_inc(h2_ready, 1)
                    dve.wait_ge(h2_ready, g + 1)
                    statistics(g, 1, ln2_stats)
                elif step == "split_w":
                    weights_lo(0, g, g + 1)
                elif step == "ln2_apply":
                    dve.wait_ge(ln2_root, g + 1)
                    if g >= 2:
                        dve.wait_ge(x2T_ps, g - 1)
                    normalize(g, 1, xn2[g % 2][:], xn2_ready)
                elif step == "ffn_low":
                    dve.wait_ge(x2_h, g + 1)
                    at = slice(g * T, (g + 1) * T)
                    nc.vector.tensor_tensor(x2_lo[:, :, at], ps_x2T[g].rearrange("p (k t) -> p k t", k=KH),
                                            x2_hi[:, :, at].bitcast(F32), ALU.subtract).then_inc(x2_l, 1)
                elif step == "read_logits":
                    if g == 0:
                        dve.wait_ge(d_late, 32)
                    dve.wait_ge(logit_ps, g + 1)
                    nc.vector.tensor_copy(logits[:, g], ps_logit[g]).then_inc(logit_ready, 1)
                    nc.vector.tensor_tensor(biased[:, g], ps_logit[g], beta_sb[:], ALU.add).then_inc(logit_ready, 1)
                elif step == "compare":
                    dve.wait_ge(logit_ready, 2 * g + 2)
                    if g >= 1:
                        dve.wait_ge(ranked, g)
                    shape = [T, EXPERTS, EXPERTS]
                    mine = biased[:, g, :, None].broadcast_to(shape)
                    other = biased[:, g, None, :].broadcast_to(shape)
                    nc.vector.tensor_tensor(greater[:], other, mine, ALU.is_gt)
                    nc.vector.tensor_tensor(equal[:], other, mine, ALU.is_equal).then_inc(compared, 1)
                elif step == "coef_copy":
                    dve.wait_ge(coefT_ps, 1)
                    nc.vector.tensor_copy(coefT[:, 3 * T:], ps_coefT[1]).then_inc(coefT_ready, 1)
                elif step == "mid":
                    mid_product(0, g)
                elif step == "next_low":
                    next_low(0, g)
                elif step == "mid_low":
                    mid_low(0, g)

            for v in range(UNITS, PAIR_UNITS):
                expert_unit(0, v)
            with dve.Fori(1, LAST_PAIR) as i:
                for v in range(PAIR_UNITS):
                    expert_unit(i, v)
            for v in range(UNITS):
                expert_unit(LAST_PAIR, v)
            dve.wait_ge(downed, (EXPERTS + 1) * UNITS)
            nc.vector.tensor_copy(result[:, 1, 1], ps_y[1][1]).then_inc(y_ready, 1)

        @block.tensor
        def _(pe):
            def product(dst, pairs):
                for i, (left, right) in enumerate(pairs):
                    last = nc.tensor.matmul(dst, left, right, start=(i == 0), stop=(i == len(pairs) - 1))
                return last

            def split(chunks, left, right):
                return [(left[a](k), right[b](k)) for k in range(chunks) for a, b in ((0, 0), (0, 1), (1, 0))]

            def embed_pairs(g):
                xh, xl = x_hi[g % XBUF], x_lo[g % XBUF]
                return split(KF, (lambda k: xh[:, k], lambda k: xl[:, k]),
                             (lambda k: tok_w[0][:, k], lambda k: tok_w[1][:, k]))

            def down_product(i, v):
                c, m = v % UNITS // MT, v % MT
                b = v // UNITS % 2
                pe.wait_ge(mid_l, i * PAIR_UNITS + v + 1)
                for hid in range(KH):
                    for w, h in ((w_hi, mid_hi), (w_hi, mid_lo), (w_lo, mid_hi)):
                        last = nc.tensor.matmul(ps_y[c][hid], down(w[b], m, hid), h[v % HBUF], start=False,
                                                stop=False, skip_group_check=True)
                last.then_inc(downed, 1)

            def gate_up_product(i, v):
                u = i * PAIR_UNITS + v
                unit = v % UNITS
                c, m = unit // MT, unit % MT
                b = v // UNITS
                chunk = slice(c * HALF, (c + 1) * HALF)
                if unit == 0:
                    pe.wait_ge(we_lo, i * (2 * PIECES) + (b + 1) * PIECES)
                if isinstance(u, int) and u == 0:
                    pe.wait_ge(exp_ready, GROUPS * KV)
                    pe.wait_ge(x2_l, -(-HALF // T))
                if isinstance(u, int) and u == 1:
                    pe.wait_ge(logit_ready, 2 * GROUPS - 4)
                if isinstance(u, int) and u == MT:
                    pe.wait_ge(x2_l, GROUPS)
                if later(i, v, 2):
                    pe.wait_ge(silu_ready, u - 1)
                    pe.wait_ge(mid_ready, u - 1)
                for matrix, dst in ((0, ps_gate), (1, ps_up)):
                    last = product(dst[v % 2],
                                   split(KH, (lambda k: gate_up(w_hi[b], matrix, k, m),
                                              lambda k: gate_up(w_lo[b], matrix, k, m)),
                                         (lambda k: x2_hi[:, k, chunk], lambda k: x2_lo[:, k, chunk])))
                last.then_inc(gu_ps, 1)

            def expert_unit(i, v):
                gate_up_product(i, v)
                down_product(i, v - LAG)

            pe.wait_ge(d_id, 16)
            for step, g in ORDER:
                if step == "embed_a":
                    if g == 0:
                        pe.wait_ge(ws_lo, 1)
                    if g >= 2:
                        pe.wait_ge(h_ready, g - 1)
                    pe.wait_ge(xs_lo, g + 1)
                    for n, (left, right) in enumerate(embed_pairs(g)[:3 * KF // 2]):
                        nc.tensor.matmul(ps_embed[g % 2], left, right, start=(n == 0), stop=False,
                                         skip_group_check=True)
                elif step == "embed_b":
                    if g == 0:
                        pe.wait_ge(ws_lo, 2)
                    rest = embed_pairs(g)[3 * KF // 2:]
                    for n, (left, right) in enumerate(rest):
                        last = nc.tensor.matmul(ps_embed[g % 2], left, right, start=False,
                                                stop=(n == len(rest) - 1), skip_group_check=True)
                    last.then_inc(embedded, 1)
                elif step == "norm_t":
                    pe.wait_ge(xn_ready, g + 1)
                    if g >= 1:
                        pe.wait_ge(xnT_l, g)
                    for k in range(KH):
                        last = nc.tensor.transpose(ps_xnT[:, k * T:(k + 1) * T], xn[:, k * P:(k + 1) * P],
                                                   id_sb[0:T, 0:T])
                    last.then_inc(xnT_ps, 1)
                elif step == "qkv":
                    if g == 0:
                        pe.wait_ge(ws_lo, 3)
                    if g >= 2:
                        pe.wait_ge(qkn_ready, g - 1)
                    pe.wait_ge(xnT_l, g + 1)
                    product(ps_qkv[g % 2], split(KH, (lambda k: xnT_hi[:, k], lambda k: xnT_lo[:, k]),
                                                 (lambda k: qkv_w[0][:, k], lambda k: qkv_w[1][:, k]))
                            ).then_inc(qkv_ps, 1)
                elif step == "heads_t":
                    pe.wait_ge(heads_l, g + 1)
                    if g >= 1:
                        pe.wait_ge(qT_ready, g)
                        pe.wait_ge(kT_ready, g)
                    blocks = heads[:].rearrange("p (b j) w -> p b (j w)", j=KV)
                    for b in range(REP + 2):
                        dst = ps_qT if b < REP else ps_kT
                        at = (b % REP) * T
                        last = nc.tensor.transpose(dst[:, at:at + T], blocks[:, b], id_sb[0:T, 0:T])
                    last.then_inc(heads_ps, 1)
                elif step == "score":
                    if g == 0:
                        pe.wait_ge(mask_ready, 1)
                        pe.wait_ge(h_ready, GROUPS)
                    if g == 2:
                        pe.wait_ge(xnT_l, GROUPS)
                    if g % KV == 0:
                        pe.wait_ge(qT_ready, g // KV + 1)
                        pe.wait_ge(k_ready, g // KV + 1)
                    if g >= SCORES:
                        pe.wait_ge(exp_ready, g - SCORES + 1)
                    k_, q_ = k_own[g // KV % 2], qT[g // KV]
                    product(ps_score[g % SCORES],
                            [(k_[:, g % KV, half], q_) for half in range(2)] +
                            [(id_r[:], mask_r[:].rearrange("p r t -> p (r t)"))]).then_inc(score_ps, 1)
                elif step == "value":
                    group, j = g // KV, g % KV
                    if g == 0:
                        pe.wait_ge(qkn_ready, GROUPS)
                    if g == KV:
                        pe.wait_ge(qT_ready, GROUPS)
                    if j == 0 and group >= 2:
                        pe.wait_ge(oT_ready, group - 1)
                    pe.wait_ge(v_ready, group + 1)
                    pe.wait_ge(exp_ready, g + 1)
                    nc.tensor.matmul(ps_value[group % 2][WIDE * j:WIDE * (j + 1), :], v_one[:, group, j],
                                     probs[g % DEEP].rearrange("p r t -> p (r t)"), start=True,
                                     stop=True).then_inc(value_ps, 1)
                elif step == "out_t":
                    pe.wait_ge(oT_ready, g + 1)
                    if g == 0:
                        pe.wait_ge(kT_ready, GROUPS)
                    else:
                        pe.wait_ge(attn_ready, g)
                    for r in range(REP):
                        last = nc.tensor.transpose(ps_out[:, r * P:(r + 1) * P], oT[:, r * T:(r + 1) * T], id_sb[:])
                    last.then_inc(out_ps, 1)
                elif step == "attn_t":
                    pe.wait_ge(attn_ready, g + 1)
                    if g >= 1:
                        pe.wait_ge(h2_ready, g)
                    flat = attn[:].rearrange("p h d -> p (h d)")
                    for k in range(KH):
                        last = nc.tensor.transpose(ps_attnT[:, k * T:(k + 1) * T], flat[:, k * P:(k + 1) * P],
                                                   id_sb[0:T, 0:T])
                    last.then_inc(attnT_ps, 1)
                elif step == "project":
                    pe.wait_ge(attnT_l, g + 1)
                    product(ps_proj, split(KH, (lambda k: attnT_hi[:, k], lambda k: attnT_lo[:, k]),
                                           (lambda k: proj_w[0][:, k], lambda k: proj_w[1][:, k]))
                            ).then_inc(proj_ps, 1)
                elif step == "seed":
                    if g == 0:
                        pe.wait_ge(oT_ready, GROUPS)
                        pe.wait_ge(logit_ready, 2 * GROUPS - 2)
                        pe.wait_ge(h2_ready, -(-HALF // T))
                    else:
                        pe.wait_ge(h2_ready, GROUPS)
                        pe.wait_ge(coefT_ready, 2)
                    for hid in range(KH):
                        first = True
                        for i in range(GROUPS):
                            lo, hi = max(i * T, g * HALF), min((i + 1) * T, (g + 1) * HALF)
                            if lo < hi:
                                nc.tensor.matmul(ps_y[g][hid][:, lo - g * HALF:hi - g * HALF],
                                                 h_all[:, i, hid * P:(hid + 1) * P],
                                                 id_sb[0:T, lo - i * T:hi - i * T], start=first, stop=False,
                                                 skip_group_check=True)
                                first = False
                elif step == "ffn_t":
                    if g == 0:
                        pe.wait_ge(qkn_ready, GROUPS)
                    elif g == GROUPS - 2:
                        pe.wait_ge(oT_ready, GROUPS - 1)
                    elif g == GROUPS - 1:
                        pe.wait_ge(attn_ready, GROUPS)
                    else:
                        pe.wait_ge(logit_ready, 2 * g)
                    pe.wait_ge(xn2_ready, g + 1)
                    for k in range(KH):
                        last = nc.tensor.transpose(ps_x2T[g][:, k * T:(k + 1) * T],
                                                   xn2[g % 2][:, k * P:(k + 1) * P], id_sb[0:T, 0:T])
                    last.then_inc(x2T_ps, 1)
                elif step == "logits":
                    pe.wait_ge(x2_l, g + 1)
                    at = slice(g * T, (g + 1) * T)
                    product(ps_logit[g], split(KH, (lambda k: x2_hi[:, k, at], lambda k: x2_lo[:, k, at]),
                                            (lambda k: gate_w[0][:, k], lambda k: gate_w[1][:, k]))
                            ).then_inc(logit_ps, 1)
                elif step == "coef_t":
                    pe.wait_ge(coef_ready, 1)
                    pe.wait_ge(attn_ready, GROUPS)
                    pe.wait_ge(h2_ready, GROUPS)
                    pe.wait_ge(logit_ready, 2 * GROUPS)
                    for i in range(GROUPS):
                        at = (i % 3) * T
                        last = nc.tensor.transpose(ps_coefT[i // 3][:, at:at + T], coef[:, i], id_sb[0:T, 0:T])
                    last.then_inc(coefT_ps, 1)
                elif step == "gate_up":
                    gate_up_product(0, g)
                elif step == "down" and g >= LAG:
                    down_product(0, g - LAG)

            for v in range(UNITS, PAIR_UNITS):
                expert_unit(0, v)
            with pe.Fori(1, LAST_PAIR) as i:
                for v in range(PAIR_UNITS):
                    expert_unit(i, v)
            for v in range(UNITS):
                expert_unit(LAST_PAIR, v)
            for v in range(UNITS - LAG, UNITS):
                down_product(LAST_PAIR, v)


def kernel(**inputs):
    import concourse.bacc as bacc
    from concourse.bass_utils import run_bass_kernel_spmd as run

    f = np.float32
    side = IMAGE // PATCH
    x = np.ascontiguousarray(inputs["x"])
    patches = x.reshape(BATCH, CHANNELS, side, PATCH, side, PATCH).transpose(0, 1, 3, 5, 2, 4)
    patches = patches.reshape(BATCH, PATCHES, FLAT).transpose(2, 0, 1)
    xt = np.zeros((FLAT, GROUPS * PER_GROUP, SEQ), f)
    xt[:, :BATCH, 1:] = patches
    xt = xt.reshape(KF, P, GROUPS, T).transpose(1, 2, 0, 3)
    clsrows = np.zeros((T, HID), f)
    clsrows[::SEQ] = inputs["cls_tok"][0, 0]

    def rows(w, k):
        return np.asarray(w).reshape(k, P, -1).transpose(1, 0, 2).reshape(P, -1)

    wq = np.asarray(inputs["L0_attn_Wq"]).reshape(KV, REP, D, HID).transpose(1, 0, 2, 3).reshape(HID, HID)
    wqkv = np.concatenate([wq, inputs["L0_attn_Wkv"]], 0).T
    wproj = np.asarray(inputs["L0_attn_Wproj"]).T.reshape(KV, REP, D, HID).transpose(1, 0, 2, 3).reshape(HID, HID)

    def expert(gate, up, dn):
        return np.concatenate([rows(gate, KH), rows(up, KH), rows(dn, MT)], 1)

    experts = np.stack([expert(inputs["L0_ffn_gate_proj_w"][e], inputs["L0_ffn_up_proj_w"][e],
                               inputs["L0_ffn_down_proj_w"][e]) for e in range(EXPERTS)])
    shared = expert(inputs["L0_ffn_shared_gate_w"][0], inputs["L0_ffn_shared_up_w"][0],
                    inputs["L0_ffn_shared_down_w"][0])
    theta = (1.0 / 10000.0 ** (np.arange(0, D, 2, dtype=f) / f(D))).astype(f)
    pos = np.tile(np.arange(SEQ, dtype=f), PER_GROUP)
    freqs = np.outer(pos, theta).astype(f)
    cos = np.concatenate([np.cos(freqs)] * 2, 1).astype(f)
    sin = np.concatenate([-np.sin(freqs), np.sin(freqs)], 1).astype(f)
    t = np.arange(T)
    mask = ((t[:, None] // SEQ == t[None] // SEQ) & (t[:, None] <= t[None]))
    mask = np.where(mask, 0.0, MASKED).astype(f)
    e = np.arange(EXPERTS)
    before = np.broadcast_to((e[None, :] < e[:, None]).astype(f), (T, EXPERTS, EXPERTS))

    arrays = {"x_in": xt, "cls_in": clsrows, "w_tok_in": rows(inputs["L0_tok_W"], KF), "w_qkv_in": rows(wqkv, KH),
              "w_proj_in": rows(wproj, KH), "w_gate_in": rows(np.asarray(inputs["L0_ffn_gate_w"]).T, KH),
              "beta_in": np.asarray(inputs["L0_ffn_beta"]), "w_exp_in": experts, "w_sh_in": shared,
              "rope_in": np.concatenate([cos, sin], 1), "mask_in": mask, "ident_in": np.eye(P, dtype=f), "before_in": before}
    arrays = {k: np.ascontiguousarray(v) for k, v in arrays.items()}
    nc = bacc.Bacc("TRN2", target_bir_lowering=False, num_devices=1)
    args = [nc.dram_tensor(k, v.shape, mybir.dt.from_np(v.dtype), kind="ExternalInput").ap()
            for k, v in arrays.items()]
    c_dram = nc.dram_tensor("coef_scratch", (EXPERTS, TOKENS), F32, kind="Internal").ap()
    out = nc.dram_tensor("out_dram", (P, KH, TOKENS), F32, kind="ExternalOutput").ap()
    vit_block(nc, *args, c_dram, out)
    r = run(nc, [arrays], core_ids=[0])
    got = r.results[0]["out_dram"]
    return np.ascontiguousarray(got.transpose(1, 0, 2).reshape(HID, BATCH, SEQ).transpose(1, 2, 0))
```
